# Optimizing a Trainium2 kernel written in Bass

```python
import numpy as np
import jax
import jax.numpy as jnp

def _softmax(x, axis=-1):
    return jax.nn.softmax(x, axis=axis)

def _gelu(x):
    return jax.nn.gelu(x, approximate=True)

def _silu(x):
    return jax.nn.silu(x)

def _sigmoid(x):
    return jax.nn.sigmoid(x)

def _layernorm(x, axis=-1, eps=1e-05):
    m = jnp.mean(x, axis=axis, keepdims=True)
    v = jnp.var(x, axis=axis, keepdims=True)
    return (x - m) / jnp.sqrt(v + eps)

def _scatter_add(tgt, idx, src, axis=0):
    return tgt.at[idx].add(src)

def _segment_sum(src, seg, n):
    return jax.ops.segment_sum(src, seg, n)
kernel_name = 'mk_macaron_d1_jaxref_r8_7b8f40'

def setup_inputs(seed: int=0):
    np.random.seed(seed)
    _w = jnp.asarray

    def _L0_attn_setup():
        import jax, jax.numpy as jnp
        import numpy as np
        B, N, D = (2, 256, 128)
        H, DH = (16, 64)
        SOFTCLAMP = 50.0
        SCALE = DH ** (-0.5)
        key = jax.random.key(seed)
        ks = jax.random.split(key, 5)
        std = D ** (-0.5)
        return {'x': jax.random.normal(ks[0], (B, N, D), dtype=jnp.float32), 'Wq': jax.random.normal(ks[1], (H * DH, D), dtype=jnp.float32) * std, 'Wk': jax.random.normal(ks[2], (H * DH, D), dtype=jnp.float32) * std, 'Wv': jax.random.normal(ks[3], (H * DH, D), dtype=jnp.float32) * std, 'Wo': jax.random.normal(ks[4], (D, H * DH), dtype=jnp.float32) * std}
    _L0_attn_in = _L0_attn_setup()

    def _L0_ffn_setup():
        import jax, jax.numpy as jnp
        import numpy as np
        EPS = 1e-08

        def _ternary_linear(x, w):
            alpha = jnp.mean(jnp.abs(w))
            w_t = jnp.sign(w) * (jnp.abs(w) > 0.5 * alpha).astype(w.dtype)
            w_q = w + jax.lax.stop_gradient(w_t - w)
            d = x.shape[-1]
            rms = jnp.sqrt(jnp.sum(x * x, axis=-1, keepdims=True)) / jnp.sqrt(jnp.asarray(d, x.dtype))
            x_norm = x / (rms + EPS)
            return jnp.einsum('bsd,fd->bsf', x_norm, w_q)
        key = jax.random.key(seed)
        k1, k2, k3 = jax.random.split(key, 3)
        d_model, d_ff = (128, 512)
        B, S = (4, 512)
        x = jax.random.normal(k1, (B, S, d_model), dtype=jnp.float32)
        w_up = jax.random.normal(k2, (d_ff, d_model), dtype=jnp.float32) * 0.02
        w_down = jax.random.normal(k3, (d_model, d_ff), dtype=jnp.float32) * 0.02
        return {'x': x, 'w_up': w_up, 'w_down': w_down}
    _L0_ffn_in = _L0_ffn_setup()
    _d = {'L0_attn_x': _L0_attn_in['x'], 'L0_attn_Wq': _L0_attn_in['Wq'], 'L0_attn_Wk': _L0_attn_in['Wk'], 'L0_attn_Wv': _L0_attn_in['Wv'], 'L0_attn_Wo': _L0_attn_in['Wo'], 'L0_ffn_w_up': _L0_ffn_in['w_up'], 'L0_ffn_w_down': _L0_ffn_in['w_down']}
    _x0 = _d['L0_attn_x']
    _d['L0_attn_x'] = jax.random.normal(jax.random.fold_in(jax.random.key(seed), 1), (1, 2048, 128), dtype=_x0.dtype)
    del _x0
    return _d

def reference(L0_attn_x, L0_attn_Wq, L0_attn_Wk, L0_attn_Wv, L0_attn_Wo, L0_ffn_w_up, L0_ffn_w_down):

    def _L0_attn_ref(x, Wq, Wk, Wv, Wo):
        import jax, jax.numpy as jnp
        import numpy as np
        B, N, D = (2, 256, 128)
        H, DH = (16, 64)
        SOFTCLAMP = 50.0
        SCALE = DH ** (-0.5)
        b, n, _ = x.shape
        q = jnp.einsum('bnd,fd->bnf', x, Wq).reshape(b, n, H, DH).transpose(0, 2, 1, 3)
        k = jnp.einsum('bnd,fd->bnf', x, Wk).reshape(b, n, H, DH).transpose(0, 2, 1, 3)
        v = jnp.einsum('bnd,fd->bnf', x, Wv).reshape(b, n, H, DH).transpose(0, 2, 1, 3)
        sim = jnp.einsum('bhid,bhjd->bhij', q, k) * SCALE
        sim = SOFTCLAMP * jnp.tanh(sim / SOFTCLAMP)
        causal = jnp.tril(jnp.ones((n, n), dtype=bool))
        sim = jnp.where(causal, sim, jnp.finfo(sim.dtype).min)
        attn = jax.nn.softmax(sim, axis=-1)
        out = jnp.einsum('bhij,bhjd->bhid', attn, v)
        out = out.transpose(0, 2, 1, 3).reshape(b, n, H * DH)
        return jnp.einsum('bnf,df->bnd', out, Wo)

    def _L0_ffn_ref(x, w_up, w_down):
        import jax, jax.numpy as jnp
        import numpy as np
        EPS = 1e-08

        def _ternary_linear(x, w):
            alpha = jnp.mean(jnp.abs(w))
            w_t = jnp.sign(w) * (jnp.abs(w) > 0.5 * alpha).astype(w.dtype)
            w_q = w + jax.lax.stop_gradient(w_t - w)
            d = x.shape[-1]
            rms = jnp.sqrt(jnp.sum(x * x, axis=-1, keepdims=True)) / jnp.sqrt(jnp.asarray(d, x.dtype))
            x_norm = x / (rms + EPS)
            return jnp.einsum('bsd,fd->bsf', x_norm, w_q)
        h = jax.nn.gelu(_ternary_linear(x, w_up), approximate=False)
        return _ternary_linear(h, w_down)
    x = L0_attn_x
    x = x + 0.5 * _L0_ffn_ref(_layernorm(x, axis=-1), L0_ffn_w_up, L0_ffn_w_down)
    x = x + _L0_attn_ref(_layernorm(x, axis=-1), L0_attn_Wq, L0_attn_Wk, L0_attn_Wv, L0_attn_Wo)
    x = x + 0.5 * _L0_ffn_ref(_layernorm(x, axis=-1), L0_ffn_w_up, L0_ffn_w_down)
    return x

_drawn_inputs = setup_inputs


def setup_inputs(seed=0):
    import zlib

    import numpy as np

    out = dict(_drawn_inputs(seed))
    spreads = {}
    factors = {}
    for name, (base, spread) in spreads.items():
        noise = np.random.default_rng([zlib.crc32(name.encode()), seed]).standard_normal(out[name].shape)
        drawn = base * np.exp(spread * noise) if base else spread * noise
        out[name] = jnp.asarray(drawn.astype(out[name].dtype))
    for name, factor in factors.items():
        out[name] = (out[name] * factor).astype(out[name].dtype)
    return out
```

```python
from contextlib import ExitStack

import concourse.bass as bass
from concourse import mybir

ALU = mybir.AluOpType
ACT = mybir.ActivationFunctionType
F32 = mybir.dt.float32
F32R = mybir.dt.float32r

P = 128
CH = 512
TPC = CH // P
LEAD = 2
ROT = 4


def causal_units(chunks):
    units = []
    for c in reversed(range(chunks)):
        units += [(c, TPC * c + k, P * k) for k in range(TPC)]
        units += [(c, jt, 0) for jt in reversed(range(TPC * c))]
    return units


def bass_macaron_block(nc: bass.Bass, x, wq, wk, wv, wo, w_up, w_down, out):
    _, N, D = x.shape
    F = w_up.shape[0]
    HDH = wq.shape[0]
    DH = 64
    PAIRS = HDH // P
    TILES = N // P
    CHUNKS = N // CH
    FT = F // P
    LN_EPS, RMS_EPS = 1e-5, 1e-8
    SOFTCLAMP = 50.0
    SCALE = DH ** -0.5
    assert D == P and N % CH == 0 and HDH % P == 0 and P == 2 * DH and F % P == 0 and CHUNKS == 4

    UNITS_OF = causal_units(CHUNKS)
    UNITS = len(UNITS_OF)
    first_unit = {c: min(u for u, x_ in enumerate(UNITS_OF) if x_[0] == c) for c in range(CHUNKS)}
    last_unit = {c: max(u for u, x_ in enumerate(UNITS_OF) if x_[0] == c) for c in range(CHUNKS)}
    rank = {c: CHUNKS - 1 - c for c in range(CHUNKS)}
    diag_rank = {}
    for u, (c, jt, _) in enumerate(UNITS_OF):
        if jt >= TPC * c:
            diag_rank[u] = len(diag_rank) + 1
    DIAGS = len(diag_rank)

    JOBS = [
        (4, "K", 0, 0), (6, "V", 0, 0), (8, "Q", 0, 0), (10, "WT", 0, 1), (12, "WoT", 0, 0),
        (14, "K", 3, 1), (16, "V", 3, 1), (17, "den", 3, 0), (18, "Q", 3, 1), (20, "out", 3, 0),
        (21, "K", 2, 1), (23, "V", 2, 1), (27, "Q", 2, 1), (29, "den", 2, 0), (31, "out", 2, 0),
        (32, "K", 1, 1), (33, "V", 1, 1), (35, "Q", 1, 1), (37, "den", 1, 0), (39, "out", 1, 0),
        (41, "den", 0, 0), (43, "out", 0, 0),
    ]
    FIRST_JOBS = [(0, "WT", 0, 0)] + [(0, j, c, 0) for c in (3, 2, 1) for j in "KVQ"]
    LAST_JOBS = [j for j in JOBS if not j[3]]
    CHAIN = {"K": 1, "Q": 1, "den": 3}
    NJ, NFJ = len(JOBS), len(FIRST_JOBS)
    NC = sum(CHAIN.get(j[1], 0) for j in JOBS)
    NFC = sum(CHAIN.get(j[1], 0) for j in FIRST_JOBS)
    assert NJ % 2 == 0 and NFJ % 2 == 0

    with ExitStack() as ctx:
        def sb(name, shape, dt=F32):
            return ctx.enter_context(nc.sbuf_tensor(name, shape, dt))

        def sem(name):
            return ctx.enter_context(nc.semaphore(name))

        psum = ctx.enter_context(nc.psum_tensor("psum", [P, 8, CH], F32))

        ident = sb("ident", [P, P])
        ones = sb("ones", [P, P])
        causal = sb("causal", [P, 2, P])
        X = sb("X", [P, TILES, D])
        w_up_nat = sb("w_up_nat", [P, FT, D])
        w_dn_nat = sb("w_dn_nat", [P, F])
        tern_neg = sb("tern_neg", [P, F])
        w_up_t = sb("w_up_t", [P, F], F32R)
        w_dn_t = sb("w_dn_t", [P, FT, D], F32R)
        abs_sum = sb("abs_sum", [P, 2])
        thr = sb("thr", [P, 4])
        stats = sb("stats", [P, TILES, 6])
        mv = sb("mv", [P, TILES, 2])
        root_in = sb("root_in", [P, 2, TILES])
        root_out = sb("root_out", [P, 2, TILES])
        small = sb("small", [P, TILES])
        scale_t = sb("scale_t", [P, TILES])
        xn = sb("xn", [P, 2, TPC, D])
        xaT = sb("xaT", [P, N])
        yT = sb("yT", [P, N])

        Qs = sb("Qs", [P, 2, N], F32R)
        K1 = sb("K1", [P, 2, N], F32R)
        K2 = sb("K2", [P, 2, N], F32R)
        V = sb("V", [P, TILES, P])
        clamped = sb("clamped", [P, 2, 2, CH])
        probs = sb("probs", [P, 4, 2, CH])
        psums = sb("psums", [P, 2, 2, CH])
        den_t = sb("den_t", [P, CH])
        den_r = sb("den_r", [P, CH // 32])
        den_b = sb("den_b", [P, CH])
        rden = sb("rden", [P, CH])
        OT = sb("OT", [P, 2, CH])
        raw_qkv = sb("raw_qkv", [P, 3, D])
        raw_o = sb("raw_o", [P, P])
        WT = sb("WT", [P, 3, P])
        WoT = sb("WoT", [P, D])

        xh = K1[:, 0, 0:2 * CH].rearrange("p (b n) -> p b n", b=2)
        xl = K1[:, 1, 0:2 * CH].rearrange("p (b n) -> p b n", b=2)
        hh = Qs[:, 0, :].rearrange("p (f n) -> p f n", f=FT)
        hl = Qs[:, 1, :].rearrange("p (f n) -> p f n", f=FT)
        h = probs[:, :, :, :].rearrange("p a b n -> p (a b) n").rearrange("p (b f) n -> p b f n", b=2)
        hsq = [clamped[:, :, :, :].rearrange("p a b n -> p (a b) n"), psums[:, :, :, :].rearrange("p a b n -> p (a b) n")]

        consts_ready = sem("consts_ready")
        x_loaded = [sem(f"x_loaded{c}") for c in range(CHUNKS)]
        ffn_w_loaded = sem("ffn_w_loaded")
        vstep = sem("vstep")
        gstep = sem("gstep")
        abs_summed = sem("abs_summed")
        thr_summed = sem("thr_summed")
        tern_ready = sem("tern_ready")
        tern_turned = sem("tern_turned")
        tern_stored = sem("tern_stored")
        root_asked = sem("root_asked")
        root_done = sem("root_done")
        xn_ready = sem("xn_ready")
        xn_turned = sem("xn_turned")
        xh_ready = sem("xh_ready")
        xl_ready = sem("xl_ready")
        up_done = sem("up_done")
        gelu_done = sem("gelu_done")
        sq_done = sem("sq_done")
        h_split = sem("h_split")
        down_done = sem("down_done")
        ss_done = sem("ss_done")
        yT_stored = sem("yT_stored")
        y_turned = sem("y_turned")
        x_updated = sem("x_updated")
        yT_cleared = sem("yT_cleared")
        xaT_stored = sem("xaT_stored")
        raw_loaded = sem("raw_loaded")
        raw_o_loaded = sem("raw_o_loaded")
        side_done = sem("side_done")
        side_taken = sem("side_taken")
        vchain = sem("vchain")
        k_swapped = sem("k_swapped")
        scored = sem("scored")
        clamp_done = sem("clamp_done")
        exp_done = sem("exp_done")
        masked = sem("masked")
        summed = sem("summed")
        pv_done = sem("pv_done")
        normed = sem("normed")
        out_stored = sem("out_stored")

        x_v = x[0].rearrange("(t p) d -> p t d", p=P)
        out_v = out[0].rearrange("(t p) d -> p t d", p=P)
        wqkv_rows = [w.rearrange("(a p) d -> a p d", p=P) for w in (wq, wk, wv)]
        wo_cols = wo.rearrange("d (a f) -> a d f", f=P)

        def S(slot):
            return psum[:, 2 * slot:2 * slot + 2, :]

        def O(q):
            return psum[:, 4 + q % 2, :]

        def side(i):
            return psum[:, 6 + i % 2, :]

        Y_BANK, SS_BANK = psum[:, 6, :], psum[:, 7, :]

        block = ctx.enter_context(nc.Block())

        @block.sync
        def _(sp):
            for c in range(CHUNKS):
                sp.dma_start(X[:, TPC * c:TPC * (c + 1), :], x_v[:, TPC * c:TPC * (c + 1), :]).then_inc(x_loaded[c], 16)
                if c == 0:
                    sp.dma_start(w_up_nat[:, :, :], w_up.rearrange("(t p) d -> p t d", p=P)).then_inc(ffn_w_loaded, 16)
                    sp.dma_start(w_dn_nat[:, :], w_down).then_inc(ffn_w_loaded, 16)

            def load_qkv(pair):
                for i, w in enumerate(wqkv_rows):
                    sp.dma_start(raw_qkv[:, i, :], w[pair]).then_inc(raw_loaded, 16)

            def swap_k(pair, c, taken):
                sp.wait_ge(side_taken, taken)
                sp.wait_ge(k_swapped, (pair * CHUNKS + rank[c]) * 32)
                cols = slice(CH * c, CH * (c + 1))
                sp.dma_start(K2[DH:P, :, cols].bitcast(F32), K1[0:DH, :, cols].bitcast(F32)).then_inc(k_swapped, 16)
                sp.dma_start(K2[0:DH, :, cols].bitcast(F32), K1[DH:P, :, cols].bitcast(F32)).then_inc(k_swapped, 16)

            load_qkv(0)
            sp.dma_start(raw_o[:, :], wo_cols[0]).then_inc(raw_o_loaded, 16)
            for i, (_, kind, c, _) in enumerate(FIRST_JOBS):
                if kind == "K":
                    swap_k(0, c, i + 1)

            def pair_loads(p, jobs):
                base = p * NJ + NFJ
                for i, (_, kind, c, nxt) in enumerate(jobs):
                    if kind == "K":
                        swap_k(p + 1 if nxt else p, c, base + i + 1)
                        if not nxt and p is not PAIRS - 1:
                            load_qkv(p + 1)
                    if kind == "WoT" and p is not PAIRS - 1:
                        sp.wait_ge(side_taken, base + i + 1)
                        sp.dma_start(raw_o[:, :], wo_cols[p + 1]).then_inc(raw_o_loaded, 16)

            with sp.Fori(0, PAIRS - 1) as p:
                pair_loads(p, JOBS)
            pair_loads(PAIRS - 1, LAST_JOBS)

            for c in range(CHUNKS):
                sp.wait_ge(x_updated, 2 * CHUNKS + 1 + c)
                sp.dma_start(out_v[:, TPC * c:TPC * (c + 1), :], X[:, TPC * c:TPC * (c + 1), :]).then_inc(out_stored, 16)
            sp.wait_ge(out_stored, 16 * CHUNKS)

        @block.tensor
        def _(pe):
            pe.wait_ge(consts_ready, 3)
            pe.wait_ge(abs_summed, 4)
            pe.matmul(SS_BANK[:, 0:2], ones[:, :], abs_sum[:, :], start=True, stop=True).then_inc(thr_summed, 1)
            pe.wait_ge(tern_ready, 2)
            for f in range(FT):
                pe.transpose(psum[:, 0, P * f:P * (f + 1)], w_up_nat[:, f, :], ident[:, :])
            for f in range(FT):
                last = pe.transpose(psum[:, 1, P * f:P * (f + 1)], w_dn_nat[:, P * f:P * (f + 1)], ident[:, :])
            last.then_inc(tern_turned, 1)
            pe.wait_ge(tern_stored, 2)

            def turn_xn(n, free):
                pe.wait_ge(xn_ready, n + 1)
                if free is not None:
                    pe.wait_ge(*free)
                for t in range(TPC):
                    last = pe.transpose(psum[:, n % 2, P * t:P * (t + 1)], xn[:, n % 2, t, :], ident[:, :])
                last.then_inc(xn_turned, 1)

            def ffn(k):
                b = CHUNKS * k

                def turn(c):
                    n = 2 * b + c
                    turn_xn(n, (xl_ready, b + c - 1) if c >= 2 else None)

                turn(0)
                for c in range(CHUNKS):
                    if c + 1 < CHUNKS:
                        turn(c + 1)
                    pe.wait_ge(xl_ready, b + c + 1)
                    pe.wait_ge(xh_ready, b + c + 1)
                    for f in range(FT):
                        if c > 0:
                            pe.wait_ge(gelu_done, FT * (b + c - 1) + f + 1)
                        bank = psum[:, 2 + f, :]
                        w = w_up_t[:, P * f:P * (f + 1)]
                        pe.matmul(bank, w, xh[:, c % 2, :], start=True, stop=False)
                        pe.matmul(bank, w, xl[:, c % 2, :], start=False, stop=True).then_inc(up_done, 1)
                    if c > 0:
                        down(b, c - 1)
                down(b, CHUNKS - 1)
                for c in range(CHUNKS):
                    turn_y(k, 2 * CHUNKS * k + c, c)

            def down(b, c):
                if c > 0:
                    pe.wait_ge(yT_stored, b + c)
                for f in range(FT):
                    pe.wait_ge(h_split, FT * (b + c) + f + 1)
                    w = w_dn_t[:, f, :]
                    pe.matmul(Y_BANK, w, hh[:, f, :], start=(f == 0), stop=False)
                    last = pe.matmul(Y_BANK, w, hl[:, f, :], start=False, stop=(f == FT - 1))
                last.then_inc(down_done, 1)
                pe.wait_ge(gstep, 3 * (b + c + 1))
                for t in range(TPC):
                    i = TPC * c + t
                    last = pe.matmul(SS_BANK[:, i:i + 1], hsq[c % 2][:, 0, P * t:P * (t + 1)], ones[:, 0:1],
                                     start=True, stop=True)
                last.then_inc(ss_done, 1)

            def turn_y(k, n, c):
                if k is not None:
                    pe.wait_ge(yT_stored, CHUNKS * k + c + 1)
                if c >= 2:
                    pe.wait_ge(x_updated, n - 1)
                for t in range(TPC):
                    last = pe.transpose(psum[:, c % 2, P * t:P * (t + 1)],
                                        yT[:, CH * c + P * t:CH * c + P * (t + 1)], ident[:, :])
                last.then_inc(y_turned, 1)

            ffn(0)
            for c in range(CHUNKS):
                turn_xn(CHUNKS + c, (xaT_stored, c - 1) if c >= 2 else None)
            pe.wait_ge(xaT_stored, CHUNKS)

            def job(i_in, base, entry, pair, first=False):
                _, kind, c, _ = entry
                bank = side(i_in)
                cols = slice(CH * c, CH * (c + 1))
                if not first:
                    pe.wait_ge(side_taken, base + i_in - 1)
                elif i_in > 0:
                    pe.wait_ge(side_taken, max(i_in - 1, 1))
                if kind in "KQ":
                    last = pe.matmul(bank, WT[:, "QKV".index(kind), :], xaT[:, cols], start=True, stop=True)
                elif kind == "V":
                    for t in range(TPC):
                        a = CH * c + P * t
                        last = pe.matmul(bank[:, P * t:P * (t + 1)], xaT[:, a:a + P], WT[:, 2, :],
                                         start=True, stop=True)
                elif kind == "WT":
                    pe.wait_ge(raw_loaded, (pair + 1) * 48)
                    for i in range(3):
                        last = pe.transpose(bank[:, P * i:P * (i + 1)], raw_qkv[:, i, :], ident[:, :])
                elif kind == "WoT":
                    pe.wait_ge(raw_o_loaded, (pair + 1) * 16)
                    last = pe.transpose(bank[:, 0:P], raw_o[:, :], ident[:, :])
                elif kind == "den":
                    pe.wait_ge(summed, pair * UNITS + last_unit[c] + 1)
                    for a in range(2):
                        last = pe.matmul(bank[DH * a:DH * (a + 1), :], ones[:, 0:DH], psums[:, rank[c] % 2, a, :],
                                         start=True, stop=True)
                elif kind == "out":
                    pe.wait_ge(normed, pair * CHUNKS + rank[c] + 1)
                    last = pe.matmul(bank, WoT[:, :], OT[:, rank[c] % 2, :], start=True, stop=True)
                last.then_inc(side_done, 1)

            def first_use(jt, c):
                return jt % TPC == (0 if jt >= TPC * c else TPC - 1)

            def score(pair, u, need=None, fresh=False):
                c, jt, off = UNITS_OF[u]
                slot = u % 2
                if not (fresh and u < 2):
                    pe.wait_ge(clamp_done, pair * UNITS + u - 1)
                if need is not None:
                    pe.wait_ge(side_taken, need)
                if c == CHUNKS - 1 and first_use(jt, c):
                    pe.wait_ge(k_swapped, (pair * CHUNKS + rank[jt // TPC] + 1) * 32)
                for a in range(2):
                    o = S(slot)[:, a, off:CH]
                    q = Qs[:, a, CH * c + off:CH * (c + 1)]
                    pe.matmul(o, K1[:, a, P * jt:P * (jt + 1)], q, start=True, stop=False)
                    last = pe.matmul(o, K2[:, a, P * jt:P * (jt + 1)], q, start=False, stop=True)
                last.then_inc(scored, 1)

            def attend(pair, u, need=None, fresh=False):
                c, jt, off = UNITS_OF[u]
                first, last_one = u == first_unit[c], u == last_unit[c]
                if u in diag_rank:
                    pe.wait_ge(masked, pair * DIAGS + diag_rank[u])
                else:
                    pe.wait_ge(exp_done, pair * UNITS + u + 1)
                if first and not fresh and rank[c] != 1:
                    pe.wait_ge(normed, pair * CHUNKS + rank[c] - 1)
                if need is not None:
                    pe.wait_ge(side_taken, need)
                for a in range(2):
                    o = O(rank[c])[DH * a:DH * (a + 1), off:CH]
                    last = pe.matmul(o, V[:, jt, DH * a:DH * (a + 1)], probs[:, u % 4, a, off:CH],
                                     start=first, stop=last_one)
                last.then_inc(pv_done, 1)

            def slot(pair, s, jobs, base, fresh=False, last=False):
                def after(kind, c, nxt):
                    return base + 1 + next(i for i, e in enumerate(jobs) if e[1:] == (kind, c, nxt))

                u = s + LEAD
                if u < UNITS:
                    need = after("K", 0, 0) if u == UNITS_OF.index((3, TPC - 1, 0)) else after("Q", 0, 0) if u == first_unit[0] else None
                    score(pair, u, need, fresh)
                elif not last:
                    need = after("Q", 3, 1) if u == UNITS else after("K", 2, 1) if u == UNITS + TPC else None
                    score(pair + 1, u - UNITS, need)
                for i, e in enumerate(jobs):
                    if e[0] == s:
                        job(i, base, e, pair + 1 if e[3] else pair)
                if s < UNITS:
                    attend(pair, s, after("V", 0, 0) if s == UNITS_OF.index((3, TPC - 1, 0)) else None, fresh)
                else:
                    attend(pair + 1, s - UNITS, after("V", 3, 1) if s == UNITS else None)

            for i, e in enumerate(FIRST_JOBS):
                job(i, 0, e, 0, first=True)
            pe.wait_ge(side_taken, NFJ)
            for u in range(LEAD):
                score(0, u, fresh=True)
            for s in range(ROT):
                slot(0, s, [], 0, fresh=True)
            with pe.Fori(0, PAIRS - 1) as p:
                for s in range(ROT, ROT + UNITS):
                    slot(p, s, JOBS, p * NJ + NFJ)
            for s in range(ROT, UNITS):
                slot(PAIRS - 1, s, LAST_JOBS, (PAIRS - 1) * NJ + NFJ, last=True)
            for i, e in enumerate(LAST_JOBS):
                if e[0] >= UNITS:
                    job(i, (PAIRS - 1) * NJ + NFJ, e, PAIRS - 1)

            pe.wait_ge(side_taken, (PAIRS - 1) * NJ + NFJ + len(LAST_JOBS))
            for c in range(CHUNKS):
                turn_y(None, CHUNKS + c, c)
            ffn(1)

        @block.scalar
        def _(act):
            def roots(n):
                act.wait_ge(root_asked, n + 1)
                act.activation(root_out[:, :, :], root_in[:, :, :], ACT.Sqrt).then_inc(root_done, 1)

            def high_part(b, c):
                act.wait_ge(xn_turned, 2 * b + c + 1)
                if c >= 2:
                    act.wait_ge(up_done, FT * (b + c - 1))
                act.copy(xh[:, c % 2, :], psum[:, c % 2, :]).then_inc(xh_ready, 1)

            def ffn(k):
                b = CHUNKS * k
                high_part(b, 0)
                for c in range(CHUNKS):
                    if c + 1 < CHUNKS:
                        high_part(b, c + 1)
                    for f in range(FT):
                        act.wait_ge(up_done, FT * (b + c) + f + 1)
                        if c >= 2:
                            act.wait_ge(h_split, FT * (b + c - 2) + f + 1)
                            act.wait_ge(sq_done, FT * (b + c - 2) + f + 1)
                        act.activation(h[:, c % 2, f, :], psum[:, 2 + f, :], ACT.Gelu).then_inc(gelu_done, 1)
                    if c > 0:
                        store_y(b, c - 1)
                    for f in range(FT):
                        act.wait_ge(gelu_done, FT * (b + c) + f + 1)
                        if c >= 2 and f == 0:
                            act.wait_ge(ss_done, b + c - 1)
                        o = hsq[c % 2][:, f, :]
                        act.activation(o, h[:, c % 2, f, :], ACT.Square).then_inc(sq_done, 1)
                store_y(b, CHUNKS - 1)

            def store_y(b, c):
                act.wait_ge(down_done, b + c + 1)
                act.copy(yT[:, CH * c:CH * (c + 1)], Y_BANK).then_inc(yT_stored, 1)

            roots(0)
            ffn(0)
            roots(1)
            roots(2)
            for c in range(CHUNKS):
                act.wait_ge(xn_turned, CHUNKS + c + 1)
                act.copy(xaT[:, CH * c:CH * (c + 1)], psum[:, c % 2, :]).then_inc(xaT_stored, 1)

            def clamp(pair, u, fresh=False):
                c, jt, off = UNITS_OF[u]
                act.wait_ge(scored, pair * UNITS + u + 1)
                if not (fresh and u < 2):
                    act.wait_ge(exp_done, pair * UNITS + u - 1)
                act.activation(clamped[:, u % 2, :, off:CH], S(u % 2)[:, :, off:CH], ACT.Tanh,
                               scale=SCALE / SOFTCLAMP).then_inc(clamp_done, 1)

            def exps(pair, u, fresh=False):
                c, jt, off = UNITS_OF[u]
                act.wait_ge(clamp_done, pair * UNITS + u + 1)
                if not (fresh and u < 4):
                    act.wait_ge(pv_done, pair * UNITS + u - 3)
                    act.wait_ge(summed, pair * UNITS + u - 3)
                act.activation(probs[:, u % 4, :, off:CH], clamped[:, u % 2, :, off:CH], ACT.Exp,
                               scale=SOFTCLAMP).then_inc(exp_done, 1)

            def slot(pair, s, fresh=False, last=False):
                if s + 1 < UNITS:
                    clamp(pair, s + 1, fresh)
                elif not last:
                    clamp(pair + 1, s + 1 - UNITS)
                exps(pair + s // UNITS, s % UNITS, fresh)

            clamp(0, 0, True)
            for s in range(ROT):
                slot(0, s, True)
            with act.Fori(0, PAIRS - 1) as p:
                for s in range(ROT, ROT + UNITS):
                    slot(p, s)
            for s in range(ROT, UNITS):
                slot(PAIRS - 1, s, last=True)

            roots(3)
            ffn(1)
            roots(4)

        @block.gpsimd
        def _(pool):
            pool.memset(ones[:, :], 1.0).then_inc(consts_ready, 1)
            pool.memset(ident[:, :], 0.0).then_inc(consts_ready, 1)
            pool.wait_ge(consts_ready, 2)
            pool.affine_select(out=ident[:, :], in_=ident[:, :], pattern=[[-1, P]], compare_op=ALU.not_equal,
                               fill=1.0, base=0, channel_multiplier=1).then_inc(consts_ready, 1)
            pool.memset(causal[:, :, :], 1.0).then_inc(consts_ready, 1)
            pool.wait_ge(consts_ready, 4)
            pool.affine_select(out=causal[:, :, :], in_=causal[:, :, :], pattern=[[0, 2], [1, P]],
                               compare_op=ALU.is_ge, fill=0.0, base=0, channel_multiplier=-1).then_inc(consts_ready, 1)
            pool.wait_ge(consts_ready, 5)

            def sum_squares(k):
                for c in range(CHUNKS):
                    n = CHUNKS * k + c
                    sq = hsq[c % 2]
                    pool.wait_ge(sq_done, FT * (n + 1))
                    pool.tensor_tensor(sq[:, 0, :], sq[:, 0, :], sq[:, 1, :], ALU.add).then_inc(gstep, 1)
                    pool.tensor_tensor(sq[:, 2, :], sq[:, 2, :], sq[:, 3, :], ALU.add).then_inc(gstep, 1)
                    pool.wait_ge(gstep, 3 * n + 2)
                    pool.tensor_tensor(sq[:, 0, :], sq[:, 0, :], sq[:, 2, :], ALU.add).then_inc(gstep, 1)

            def mask(pair, u):
                c, jt, off = UNITS_OF[u]
                pool.wait_ge(exp_done, pair * UNITS + u + 1)
                tile = probs[:, u % 4, :, off:off + P]
                pool.tensor_tensor(tile, tile, causal[:, :, :], ALU.mult).then_inc(masked, 1)

            sum_squares(0)
            for s in range(ROT):
                mask(0, s)
            with pool.Fori(0, PAIRS - 1) as p:
                for s in range(ROT, ROT + UNITS):
                    if s % UNITS in diag_rank:
                        mask(p + s // UNITS, s % UNITS)
            for s in range(ROT, UNITS):
                if s in diag_rank:
                    mask(PAIRS - 1, s)
            sum_squares(1)

        @block.vector
        def _(dve):
            steps = [0]

            def step(ins):
                steps[0] += 1
                ins.then_inc(vstep, 1)
                dve.wait_ge(vstep, steps[0])

            dve.wait_ge(ffn_w_loaded, 32)
            w_up_flat = w_up_nat[:, :, :].rearrange("p t d -> p (t d)")
            for i, w in enumerate((w_up_flat, w_dn_nat[:, :])):
                dve.scalar_tensor_tensor(tern_neg[:, :], w, -1.0, w, ALU.mult, ALU.max).then_inc(abs_summed, 1)
                dve.wait_ge(abs_summed, 2 * i + 1)
                dve.tensor_reduce(abs_sum[:, i:i + 1], tern_neg[:, :], mybir.AxisListType.X,
                                  ALU.add).then_inc(abs_summed, 1)
                dve.wait_ge(abs_summed, 2 * i + 2)
            dve.wait_ge(thr_summed, 1)
            dve.tensor_scalar(thr[:, 0:2], SS_BANK[:, 0:2], 0.5 / (F * D), None, ALU.mult)
            step(dve.tensor_scalar(thr[:, 2:4], SS_BANK[:, 0:2], -0.5 / (F * D), None, ALU.mult))
            for i, w in enumerate((w_up_flat, w_dn_nat[:, :])):
                step(dve.tensor_scalar(tern_neg[:, :], w, thr[:, 2 + i:3 + i], None, ALU.is_lt))
                dve.scalar_tensor_tensor(w, w, thr[:, i:i + 1], tern_neg[:, :], ALU.is_gt,
                                         ALU.subtract).then_inc(tern_ready, 1)
                dve.wait_ge(tern_ready, i + 1)
            dve.wait_ge(tern_turned, 1)
            dve.tensor_copy(w_up_t[:, :], psum[:, 0, :]).then_inc(tern_stored, 1)
            dve.tensor_copy(w_dn_t[:, :, :].rearrange("p t d -> p (t d)"), psum[:, 1, :]).then_inc(tern_stored, 1)
            dve.memset(yT[:, :], 0.0).then_inc(yT_cleared, 1)

            def statistics(c):
                for t in range(TPC * c, TPC * (c + 1)):
                    ins = dve.bn_stats(stats[:, t, :], X[:, t, :])
                step(ins)
                for t in range(TPC * c, TPC * (c + 1)):
                    ins = dve.bn_aggr(mv[:, t, :], stats[:, t, :])
                step(ins)

            def norm_scale(n, with_rms):
                step(dve.tensor_scalar(root_in[:, 0, :], mv[:, :, 1], LN_EPS, None, ALU.add))
                if with_rms:
                    step(dve.reciprocal(small[:, :], root_in[:, 0, :]))
                    ins = dve.tensor_tensor(root_in[:, 1, :], small[:, :], mv[:, :, 1], ALU.mult)
                else:
                    ins = dve.tensor_copy(root_in[:, 1, :], root_in[:, 0, :])
                ins.then_inc(root_asked, 1)
                dve.wait_ge(root_done, n + 1)
                if with_rms:
                    step(dve.scalar_tensor_tensor(small[:, :], root_out[:, 1, :], RMS_EPS, root_out[:, 0, :],
                                                  ALU.add, ALU.mult))
                    step(dve.reciprocal(scale_t[:, :], small[:, :]))
                else:
                    step(dve.reciprocal(scale_t[:, :], root_out[:, 0, :]))

            def normalise(n, c):
                if n >= 2:
                    dve.wait_ge(xn_turned, n - 1)
                for t in range(TPC):
                    i = TPC * c + t
                    ins = dve.tensor_scalar(xn[:, n % 2, t, :], X[:, i, :], mv[:, i, 0:1], scale_t[:, i:i + 1],
                                            ALU.subtract, ALU.mult)
                ins.then_inc(xn_ready, 1)

            def low_part(b, c):
                dve.wait_ge(xh_ready, b + c + 1)
                if c >= 2:
                    dve.wait_ge(up_done, FT * (b + c - 1))
                dve.tensor_tensor(xl[:, c % 2, :], psum[:, c % 2, :], xh[:, c % 2, :].bitcast(F32),
                                  ALU.subtract).then_inc(xl_ready, 1)

            def ffn(k, n_root):
                b = CHUNKS * k
                n = 2 * b
                normalise(n, 0)
                normalise(n + 1, 1)
                low_part(b, 0)
                for c in range(CHUNKS):
                    if c + 1 < CHUNKS:
                        low_part(b, c + 1)
                    if c + 2 < CHUNKS:
                        normalise(n + c + 2, c + 2)
                    if c > 0:
                        dve.wait_ge(down_done, b + c)
                    for f in range(FT):
                        dve.wait_ge(gelu_done, FT * (b + c) + f + 1)
                        step(dve.tensor_copy(hh[:, f, :], h[:, c % 2, f, :]))
                        dve.tensor_tensor(hl[:, f, :], h[:, c % 2, f, :], hh[:, f, :].bitcast(F32),
                                          ALU.subtract).then_inc(h_split, 1)
                dve.wait_ge(ss_done, b + CHUNKS)
                dve.tensor_scalar(root_in[:, 0, :], SS_BANK[:, 0:TILES], 1.0 / F, None,
                                  ALU.mult).then_inc(root_asked, 1)
                dve.wait_ge(root_done, n_root + 1)
                step(dve.tensor_scalar(small[:, :], root_out[:, 0, :], RMS_EPS, 2.0, ALU.add, ALU.mult))
                step(dve.reciprocal(scale_t[:, :], small[:, :]))
                for c in range(CHUNKS):
                    dve.wait_ge(y_turned, n + c + 1)
                    for t in range(TPC):
                        i = TPC * c + t
                        ins = dve.scalar_tensor_tensor(X[:, i, :], psum[:, c % 2, P * t:P * (t + 1)],
                                                       scale_t[:, i:i + 1], X[:, i, :], ALU.mult, ALU.add)
                    ins.then_inc(x_updated, 1)

            for c in range(CHUNKS):
                dve.wait_ge(x_loaded[c], 16)
                statistics(c)
            norm_scale(0, True)
            ffn(0, 1)
            dve.wait_ge(x_updated, CHUNKS)
            for c in range(CHUNKS):
                statistics(c)
            norm_scale(2, False)
            for c in range(CHUNKS):
                normalise(CHUNKS + c, c)
            dve.memset(yT[:, :], 0.0).then_inc(yT_cleared, 1)

            def split(bank, c, T, chain):
                cols = slice(CH * c, CH * (c + 1))
                lo, hi = slice(0, DH), slice(DH, P)
                dve.tensor_copy(T[lo, 0, cols], bank[lo, :])
                dve.tensor_copy(T[hi, 1, cols], bank[hi, :]).then_inc(vchain, 1)
                dve.wait_ge(vchain, chain + 1)
                dve.tensor_tensor(T[hi, 0, cols], bank[lo, :], T[lo, 0, cols].bitcast(F32), ALU.subtract)
                return dve.tensor_tensor(T[lo, 1, cols], bank[hi, :], T[hi, 1, cols].bitcast(F32), ALU.subtract)

            def last_use(pair, units):
                return pair * UNITS + 1 if units == UNITS else (pair - 1) * UNITS + units

            def take(i, base, entry, pair, chain, first=False):
                _, kind, c, _ = entry
                bank = side(i)
                cols = slice(CH * c, CH * (c + 1))
                dve.wait_ge(side_done, base + i + 1)
                if kind == "K":
                    if not first:
                        dve.wait_ge(scored, last_use(pair, first_unit[c] + TPC))
                    split(bank, c, K1, chain).then_inc(side_taken, 1)
                elif kind == "Q":
                    if not first:
                        dve.wait_ge(scored, last_use(pair, last_unit[c] + 1))
                    split(bank, c, Qs, chain).then_inc(side_taken, 1)
                elif kind == "V":
                    if not first:
                        dve.wait_ge(pv_done, last_use(pair, first_unit[c] + TPC))
                    dve.tensor_copy(V[:, TPC * c:TPC * (c + 1), :].rearrange("p t f -> p (t f)"),
                                    bank).then_inc(side_taken, 1)
                elif kind == "WT":
                    dve.tensor_copy(WT[:, :, :].rearrange("p i f -> p (i f)"), bank[:, 0:3 * P]).then_inc(side_taken, 1)
                elif kind == "WoT":
                    dve.tensor_copy(WoT[:, :], bank[:, 0:P]).then_inc(side_taken, 1)
                elif kind == "den":
                    dve.transpose(den_t[:, :], bank).then_inc(side_taken, 1)
                    dve.wait_ge(side_taken, base + i + 1)
                    own = den_t[:, :].rearrange("p (b k) -> p b k", k=32)
                    dve.reciprocal(den_r[:, :], own[:, :, 0]).then_inc(vchain, 1)
                    dve.wait_ge(vchain, chain + 1)
                    dve.tensor_copy(den_b[:, :].rearrange("p (b k) -> p b k", k=32),
                                    den_r[:, :].unsqueeze(2).broadcast_to([P, CH // 32, 32])).then_inc(vchain, 1)
                    dve.wait_ge(vchain, chain + 2)
                    dve.transpose(rden[:, :], den_b[:, :]).then_inc(vchain, 1)
                    dve.wait_ge(vchain, chain + 3)
                    dve.wait_ge(pv_done, pair * UNITS + last_unit[c] + 1)
                    dve.tensor_tensor(OT[:, rank[c] % 2, :], O(rank[c]), rden[:, :], ALU.mult).then_inc(normed, 1)
                elif kind == "out":
                    dve.tensor_tensor(yT[:, cols], bank, yT[:, cols], ALU.add).then_inc(side_taken, 1)

            def add_probs(pair, u):
                c, jt, off = UNITS_OF[u]
                if u in diag_rank:
                    dve.wait_ge(masked, pair * DIAGS + diag_rank[u])
                else:
                    dve.wait_ge(exp_done, pair * UNITS + u + 1)
                dve.wait_ge(summed, pair * UNITS + u)
                total = psums[:, rank[c] % 2, :, off:CH]
                new = probs[:, u % 4, :, off:CH]
                if u == first_unit[c]:
                    dve.tensor_copy(total, new).then_inc(summed, 1)
                else:
                    dve.tensor_tensor(total, total, new, ALU.add).then_inc(summed, 1)

            def chain_before(jobs, i):
                return sum(CHAIN.get(e[1], 0) for e in jobs[:i])

            def slot(pair, s, jobs, base, chain):
                for i, e in enumerate(jobs):
                    if e[0] == s:
                        take(i, base, e, pair + 1 if e[3] else pair, chain + chain_before(jobs, i))
                if s < UNITS:
                    add_probs(pair, s)
                elif s < UNITS + ROT and jobs is not LAST_JOBS:
                    add_probs(pair + 1, s - UNITS)

            for i, e in enumerate(FIRST_JOBS):
                take(i, 0, e, 0, chain_before(FIRST_JOBS, i), first=True)
            for s in range(ROT):
                slot(0, s, [], 0, 0)
            with dve.Fori(0, PAIRS - 1) as p:
                for s in range(ROT, ROT + UNITS):
                    slot(p, s, JOBS, p * NJ + NFJ, p * NC + NFC)
            for s in range(ROT, UNITS + ROT):
                slot(PAIRS - 1, s, LAST_JOBS, (PAIRS - 1) * NJ + NFJ, (PAIRS - 1) * NC + NFC)

            for c in range(CHUNKS):
                dve.wait_ge(y_turned, CHUNKS + c + 1)
                dve.tensor_tensor(X[:, TPC * c:TPC * (c + 1), :].rearrange("p t d -> p (t d)"), psum[:, c % 2, :],
                                  X[:, TPC * c:TPC * (c + 1), :].rearrange("p t d -> p (t d)"),
                                  ALU.add).then_inc(x_updated, 1)
                dve.wait_ge(x_updated, CHUNKS + c + 1)
                statistics(c)
            norm_scale(3, True)
            ffn(1, 4)


_INS = ["L0_attn_x", "L0_attn_Wq", "L0_attn_Wk", "L0_attn_Wv", "L0_attn_Wo", "L0_ffn_w_up", "L0_ffn_w_down"]


def kernel(**inputs):
    import numpy as _np
    import concourse.bacc as _bacc
    from concourse import mybir as _mybir
    from concourse.bass_utils import run_bass_kernel_spmd as _run

    nc = _bacc.Bacc("TRN2", target_bir_lowering=False, num_devices=1)
    arrays, args = {}, []
    for name in _INS:
        a = _np.ascontiguousarray(inputs[name])
        arrays[f"in_{name}_dram"] = a
        args.append(nc.dram_tensor(f"in_{name}_dram", a.shape, _mybir.dt.from_np(a.dtype), kind="ExternalInput").ap())
    shape = tuple(inputs["L0_attn_x"].shape)
    args.append(nc.dram_tensor("out_0_dram", shape, _mybir.dt.float32, kind="ExternalOutput").ap())
    bass_macaron_block(nc, *args)
    r = _run(nc, [arrays], core_ids=[0])
    return r.results[0]["out_0_dram"]
```

```python
from contextlib import ExitStack

import concourse.bass as bass
from concourse import mybir

ALU = mybir.AluOpType
ACT = mybir.ActivationFunctionType
F32 = mybir.dt.float32
F32R = mybir.dt.float32r

P = 128
CH = 512
TPC = CH // P
LEAD = 4
AHEAD = 2
PBUF = 5
ROT = 14


def causal_units(chunks):
    units = []
    for c in reversed(range(chunks)):
        units += [(c, TPC * c + k, P * k) for k in range(TPC)]
        units += [(c, jt, 0) for jt in reversed(range(TPC * c))]
    return units


def bass_macaron_block(nc: bass.Bass, x, wq, wk, wv, wo, w_up, w_down, out):
    _, N, D = x.shape
    F = w_up.shape[0]
    HDH = wq.shape[0]
    DH = 64
    PAIRS = HDH // P
    TILES = N // P
    CHUNKS = N // CH
    FT = F // P
    LN_EPS, RMS_EPS = 1e-5, 1e-8
    SOFTCLAMP = 50.0
    SCALE = DH ** -0.5
    assert D == P and N % CH == 0 and HDH % P == 0 and P == 2 * DH and F % P == 0 and CHUNKS == 4

    UNITS_OF = causal_units(CHUNKS)
    UNITS = len(UNITS_OF)
    first_unit = {c: min(u for u, x_ in enumerate(UNITS_OF) if x_[0] == c) for c in range(CHUNKS)}
    last_unit = {c: max(u for u, x_ in enumerate(UNITS_OF) if x_[0] == c) for c in range(CHUNKS)}
    rank = {c: CHUNKS - 1 - c for c in range(CHUNKS)}
    diag_rank = {}
    for u, (c, jt, _) in enumerate(UNITS_OF):
        if jt >= TPC * c:
            diag_rank[u] = len(diag_rank) + 1
    DIAGS = len(diag_rank)
    POOL_SUMS = (7, 9, 12, 14, 20, 22, 24, 26, 32, 34)

    JOBS = [
        (14, "WT", 0, 1), (16, "WoT", 0, 0), (17, "K", 3, 1), (18, "den", 3, 0), (19, "V", 3, 1), (21, "out", 3, 0),
        (22, "Q", 3, 1), (24, "K", 2, 1), (26, "V", 2, 1), (30, "den", 2, 0), (31, "K", 1, 1), (33, "out", 2, 0),
        (34, "V", 1, 1), (35, "Q", 2, 1), (37, "Q", 1, 1), (38, "den", 1, 0), (40, "K", 0, 1), (42, "den", 0, 0),
        (43, "out", 1, 0), (45, "V", 0, 1), (46, "out", 0, 0), (50, "Q", 0, 1),
    ]
    FIRST_JOBS = [(-1, "xa", 3, 0), (-1, "WT", 0, 0), (-1, "xa", 2, 0), (-1, "K", 3, 0), (-1, "Q", 3, 0),
                  (-1, "K", 2, 0), (-1, "xa", 1, 0), (-1, "V", 3, 0), (-1, "K", 1, 0), (0, "xa", 0, 0),
                  (2, "V", 2, 0), (3, "K", 0, 0), (6, "V", 1, 0), (9, "Q", 2, 0), (10, "V", 0, 0), (12, "Q", 1, 0), (13, "Q", 0, 0)]
    LAST_JOBS = [(16, "WoT", 0, 0), (18, "den", 3, 0), (21, "out", 3, 0), (24, "fin", 3, 0), (30, "den", 2, 0),
                 (33, "out", 2, 0), (36, "fin", 2, 0), (38, "den", 1, 0), (UNITS, "out", 1, 0), (UNITS, "den", 0, 0),
                 (UNITS, "fin", 1, 0), (UNITS, "out", 0, 0), (UNITS, "fin", 0, 0)]
    ORDER = list(reversed(range(CHUNKS)))
    CHAIN = {"K": 1, "Q": 1, "WT": 1, "den": 3}
    NJ, NFJ = len(JOBS), len(FIRST_JOBS)
    NC = sum(CHAIN.get(j[1], 0) for j in JOBS)
    NFC = sum(CHAIN.get(j[1], 0) for j in FIRST_JOBS)
    assert NJ % 2 == 0 and len(JOBS) == len(LAST_JOBS) + 9 and JOBS == sorted(JOBS, key=lambda j: j[0])

    with ExitStack() as ctx:
        def sb(name, shape, dt=F32):
            return ctx.enter_context(nc.sbuf_tensor(name, shape, dt))

        def sem(name):
            return ctx.enter_context(nc.semaphore(name))

        psum = ctx.enter_context(nc.psum_tensor("psum", [P, 8, CH], F32))

        ident = sb("ident", [P, P])
        ones = sb("ones", [P, P])
        causal = sb("causal", [P, 2, P])
        X = sb("X", [P, TILES, D])
        w_up_nat = sb("w_up_nat", [P, FT, D])
        w_dn_nat = sb("w_dn_nat", [P, F])
        tern_neg = sb("tern_neg", [P, F])
        w_up_t = sb("w_up_t", [P, F], F32R)
        w_dn_t = sb("w_dn_t", [P, FT, D], F32R)
        abs_sum = sb("abs_sum", [P, 2])
        thr = sb("thr", [P, 4])
        stats = sb("stats", [P, TILES, 6])
        mv = sb("mv", [P, TILES, 2])
        root_in = sb("root_in", [P, 2, TILES])
        root_out = sb("root_out", [P, 2, TILES])
        small = sb("small", [P, TILES])
        scale_t = sb("scale_t", [P, TILES])
        shift_t = sb("shift_t", [P, TILES])
        xn = sb("xn", [P, 4, TPC, D])
        xaT = sb("xaT", [P, N])
        yT = sb("yT", [P, N])

        Qs = sb("Qs", [P, 2, N], F32R)
        K1 = sb("K1", [P, 2, N], F32R)
        K2 = sb("K2", [P, 2, N], F32R)
        V = sb("V", [P, TILES, P])
        clamped = sb("clamped", [P, 2, 2, CH])
        probs = sb("probs", [P, PBUF, 2, CH])
        psums = sb("psums", [P, 2, 2, CH])
        den_t = sb("den_t", [P, CH])
        den_r = sb("den_r", [P, CH // 32])
        den_b = sb("den_b", [P, CH])
        rden = sb("rden", [P, CH])
        OT = sb("OT", [P, 2, CH])
        raw_qkv = sb("raw_qkv", [P, 3, D])
        raw_o = sb("raw_o", [P, P])
        WTh = sb("WTh", [P, 2, P], F32R)
        WTl = sb("WTl", [P, 2, P], F32R)
        WvT = sb("WvT", [P, P])
        xah = sb("xah", [P, N], F32R)
        xal = sb("xal", [P, N], F32R)
        WoT = sb("WoT", [P, D])

        xh = K1[:, 0, 0:2 * CH].rearrange("p (b n) -> p b n", b=2)
        xl = K1[:, 1, 0:2 * CH].rearrange("p (b n) -> p b n", b=2)
        hh, hl = ([T[:, part, :].rearrange("p (f n) -> p f n", f=FT) for T in (Qs, K2)] for part in range(2))
        h = probs[:, 0:4, :, :].rearrange("p a b n -> p (a b) n").rearrange("p (b f) n -> p b f n", b=2)
        hsq = [clamped[:, :, :, :].rearrange("p a b n -> p (a b) n"), psums[:, :, :, :].rearrange("p a b n -> p (a b) n")]

        consts_ready = sem("consts_ready")
        x_loaded = [sem(f"x_loaded{c}") for c in range(CHUNKS)]
        ffn_w_loaded = sem("ffn_w_loaded")
        vstep = sem("vstep")
        gstep = sem("gstep")
        abs_summed = sem("abs_summed")
        thr_summed = sem("thr_summed")
        tern_ready = sem("tern_ready")
        tern_turned = sem("tern_turned")
        tern_stored = sem("tern_stored")
        root_asked = sem("root_asked")
        root_done = sem("root_done")
        xn_ready = sem("xn_ready")
        xn_turned = sem("xn_turned")
        xh_ready = sem("xh_ready")
        xl_ready = sem("xl_ready")
        up_done = sem("up_done")
        gelu_done = sem("gelu_done")
        sq_done = sem("sq_done")
        h_split = sem("h_split")
        down_done = sem("down_done")
        ss_done = sem("ss_done")
        yT_stored = sem("yT_stored")
        y_turned = sem("y_turned")
        x_updated = sem("x_updated")
        yT_cleared = sem("yT_cleared")
        scale_ready = sem("scale_ready")
        xa_ready = sem("xa_ready")
        xah_stored = sem("xah_stored")
        xaT_stored = sem("xaT_stored")
        raw_loaded = sem("raw_loaded")
        raw_o_loaded = sem("raw_o_loaded")
        side_done = sem("side_done")
        side_taken = sem("side_taken")
        vchain = sem("vchain")
        k_swapped = sem("k_swapped")
        scored = sem("scored")
        clamp_done = sem("clamp_done")
        exp_done = sem("exp_done")
        masked = sem("masked")
        summed = sem("summed")
        pv_done = sem("pv_done")
        normed = sem("normed")
        out_stored = sem("out_stored")

        x_v = x[0].rearrange("(t p) d -> p t d", p=P)
        out_v = out[0].rearrange("(t p) d -> p t d", p=P)
        wqkv_rows = [w.rearrange("(a p) d -> a p d", p=P) for w in (wq, wk, wv)]
        wo_cols = wo.rearrange("d (a f) -> a d f", f=P)

        def S(slot):
            return psum[:, 2 * slot:2 * slot + 2, :]

        def O(q):
            return psum[:, 4 + q % 2, :]

        def side(i, first=False):
            return psum[:, 6 + (i if first else i + NFJ) % 2, :]

        Y_BANK, SS_BANK = psum[:, 6, :], psum[:, 7, :]

        block = ctx.enter_context(nc.Block())

        @block.sync
        def _(sp):
            for c in range(CHUNKS):
                sp.dma_start(X[:, TPC * c:TPC * (c + 1), :], x_v[:, TPC * c:TPC * (c + 1), :]).then_inc(x_loaded[c], 16)

            def load_qkv(pair):
                for i, w in enumerate(wqkv_rows):
                    sp.dma_start(raw_qkv[:, i, :], w[pair]).then_inc(raw_loaded, 16)

            def swap_k(pair, c, taken):
                sp.wait_ge(side_taken, taken)
                sp.wait_ge(k_swapped, (pair * CHUNKS + rank[c]) * 32)
                cols = slice(CH * c, CH * (c + 1))
                sp.dma_start(K2[DH:P, :, cols].bitcast(F32), K1[0:DH, :, cols].bitcast(F32)).then_inc(k_swapped, 16)
                sp.dma_start(K2[0:DH, :, cols].bitcast(F32), K1[DH:P, :, cols].bitcast(F32)).then_inc(k_swapped, 16)

            load_qkv(0)
            sp.dma_start(raw_o[:, :], wo_cols[0]).then_inc(raw_o_loaded, 16)
            for i, (_, kind, c, _) in enumerate(FIRST_JOBS):
                if kind == "K":
                    swap_k(0, c, i + 1)

            with sp.Fori(0, PAIRS - 1) as p:
                load_qkv(p + 1)
                for i, (_, kind, c, nxt) in enumerate(JOBS):
                    if kind == "K":
                        swap_k(p + 1, c, p * NJ + NFJ + i + 1)
                    if kind == "WoT":
                        sp.wait_ge(side_taken, p * NJ + NFJ + i + 1)
                        sp.dma_start(raw_o[:, :], wo_cols[p + 1]).then_inc(raw_o_loaded, 16)

            for r, c in enumerate(ORDER):
                sp.wait_ge(x_updated, CHUNKS + 1 + r)
                sp.dma_start(out_v[:, TPC * c:TPC * (c + 1), :], X[:, TPC * c:TPC * (c + 1), :]).then_inc(out_stored, 16)
            sp.wait_ge(out_stored, 16 * CHUNKS)

        @block.tensor
        def _(pe):
            pe.wait_ge(consts_ready, 3)
            pe.wait_ge(abs_summed, 4)
            pe.matmul(SS_BANK[:, 0:2], ones[:, :], abs_sum[:, :], start=True, stop=True).then_inc(thr_summed, 1)
            pe.wait_ge(tern_ready, 2)
            for f in range(FT):
                pe.transpose(psum[:, 0, P * f:P * (f + 1)], w_up_nat[:, f, :], ident[:, :])
            for f in range(FT):
                last = pe.transpose(psum[:, 1, P * f:P * (f + 1)], w_dn_nat[:, P * f:P * (f + 1)], ident[:, :])
            last.then_inc(tern_turned, 1)
            pe.wait_ge(tern_stored, 2)

            def turn_xn(n, free):
                pe.wait_ge(xn_ready, n + 1)
                if free is not None:
                    pe.wait_ge(*free)
                for t in range(TPC):
                    last = pe.transpose(psum[:, n % 2, P * t:P * (t + 1)], xn[:, n % 2, t, :], ident[:, :])
                last.then_inc(xn_turned, 1)

            def ffn(k):
                b = CHUNKS * k

                def turn(c):
                    n = b + c
                    turn_xn(n, (xl_ready, b + c - 1) if c >= 2 else None)

                turn(0)
                for c in range(CHUNKS):
                    if c + 1 < CHUNKS:
                        turn(c + 1)
                    pe.wait_ge(xl_ready, b + c + 1)
                    pe.wait_ge(xh_ready, b + c + 1)
                    for f in range(FT):
                        if c > 0:
                            pe.wait_ge(gelu_done, FT * (b + c - 1) + f + 1)
                        bank = psum[:, 2 + f, :]
                        w = w_up_t[:, P * f:P * (f + 1)]
                        pe.matmul(bank, w, xh[:, c % 2, :], start=True, stop=False)
                        pe.matmul(bank, w, xl[:, c % 2, :], start=False, stop=True).then_inc(up_done, 1)
                    if c > 0:
                        down(b, c - 1)
                    if c > 1:
                        sum_h(b, c - 2)
                down(b, CHUNKS - 1)
                sum_h(b, CHUNKS - 2)
                sum_h(b, CHUNKS - 1)
                for r in range(CHUNKS):
                    turn_y(b, r)

            def down(b, c):
                if c > 0:
                    pe.wait_ge(yT_stored, b + c)
                for f in range(FT):
                    pe.wait_ge(h_split, FT * (b + c) + f + 1)
                    w = w_dn_t[:, f, :]
                    pe.matmul(Y_BANK, w, hh[c % 2][:, f, :], start=(f == 0), stop=False)
                    last = pe.matmul(Y_BANK, w, hl[c % 2][:, f, :], start=False, stop=(f == FT - 1))
                last.then_inc(down_done, 1)

            def sum_h(b, c):
                pe.wait_ge(gstep, 3 * (b + c + 1))
                for t in range(TPC):
                    i = TPC * c + t
                    last = pe.matmul(SS_BANK[:, i:i + 1], hsq[c % 2][:, 0, P * t:P * (t + 1)], ones[:, 0:1],
                                     start=True, stop=True)
                last.then_inc(ss_done, 1)

            def turn_y(b, r):
                c = ORDER[r]
                pe.wait_ge(yT_stored, b + c + 1)
                if r >= 2:
                    pe.wait_ge(x_updated, b + r - 1)
                turn_tokens(psum[:, r % 2, :], c).then_inc(y_turned, 1)

            def turn_tokens(bank, c):
                for t in range(TPC):
                    last = pe.transpose(bank[:, P * t:P * (t + 1)],
                                        yT[:, CH * c + P * t:CH * c + P * (t + 1)], ident[:, :])
                return last

            ffn(0)

            def job(i_in, base, entry, pair, first=False):
                _, kind, c, _ = entry
                bank = side(i_in, first)
                cols = slice(CH * c, CH * (c + 1))
                if not first:
                    pe.wait_ge(side_taken, base + i_in - 1)
                elif i_in > 1:
                    pe.wait_ge(side_taken, i_in - 1)
                if kind in "KQ":
                    w = slice("QK".index(kind), "QK".index(kind) + 1)
                    pe.matmul(bank, WTh[:, w, :], xah[:, cols], start=True, stop=False)
                    pe.matmul(bank, WTh[:, w, :], xal[:, cols], start=False, stop=False)
                    last = pe.matmul(bank, WTl[:, w, :], xah[:, cols], start=False, stop=True)
                elif kind == "V":
                    for t in range(TPC):
                        a = CH * c + P * t
                        last = pe.matmul(bank[:, P * t:P * (t + 1)], xaT[:, a:a + P], WvT[:, :],
                                         start=True, stop=True)
                elif kind == "WT":
                    pe.wait_ge(raw_loaded, (pair + 1) * 48)
                    for i in range(3):
                        last = pe.transpose(bank[:, P * i:P * (i + 1)], raw_qkv[:, i, :], ident[:, :])
                elif kind == "WoT":
                    pe.wait_ge(raw_o_loaded, (pair + 1) * 16)
                    last = pe.transpose(bank[:, 0:P], raw_o[:, :], ident[:, :])
                elif kind == "xa":
                    pe.wait_ge(xa_ready, rank[c] + 1)
                    for t in range(TPC):
                        last = pe.transpose(bank[:, P * t:P * (t + 1)], xn[:, rank[c], t, :], ident[:, :])
                elif kind == "fin":
                    out_i = next(i for i, e in enumerate(LAST_JOBS) if e[1:3] == ("out", c))
                    pe.wait_ge(side_taken, base + out_i + 1)
                    last = turn_tokens(bank, c)
                elif kind == "den":
                    pe.wait_ge(summed, pair * UNITS + last_unit[c] + 1)
                    for a in range(2):
                        last = pe.matmul(bank[DH * a:DH * (a + 1), :], ones[:, 0:DH], psums[:, rank[c] % 2, a, :],
                                         start=True, stop=True)
                elif kind == "out":
                    pe.wait_ge(normed, pair * CHUNKS + rank[c] + 1)
                    last = pe.matmul(bank, WoT[:, :], OT[:, rank[c] % 2, :], start=True, stop=True)
                last.then_inc(side_done, 1)

            def first_use(jt, c):
                return jt % TPC == (0 if jt >= TPC * c else TPC - 1)

            def score(pair, u, need=None, fresh=False):
                c, jt, off = UNITS_OF[u]
                slot = u % 2
                if not (fresh and u < 2):
                    pe.wait_ge(clamp_done, pair * UNITS + u - 1)
                if need is not None:
                    pe.wait_ge(side_taken, need)
                if c == CHUNKS - 1 and first_use(jt, c):
                    pe.wait_ge(k_swapped, (pair * CHUNKS + rank[jt // TPC] + 1) * 32)
                for a in range(2):
                    o = S(slot)[:, a, off:CH]
                    q = Qs[:, a, CH * c + off:CH * (c + 1)]
                    pe.matmul(o, K1[:, a, P * jt:P * (jt + 1)], q, start=True, stop=False)
                    last = pe.matmul(o, K2[:, a, P * jt:P * (jt + 1)], q, start=False, stop=True)
                last.then_inc(scored, 1)

            def attend(pair, u, need=None, fresh=False):
                c, jt, off = UNITS_OF[u]
                first, last_one = u == first_unit[c], u == last_unit[c]
                if u in diag_rank:
                    pe.wait_ge(masked, pair * DIAGS + diag_rank[u])
                else:
                    pe.wait_ge(exp_done, pair * UNITS + u + 1)
                if first and not fresh and rank[c] != 1:
                    pe.wait_ge(normed, pair * CHUNKS + rank[c] - 1)
                if need is not None:
                    pe.wait_ge(side_taken, need)
                for a in range(2):
                    o = O(rank[c])[DH * a:DH * (a + 1), off:CH]
                    last = pe.matmul(o, V[:, jt, DH * a:DH * (a + 1)], probs[:, u % PBUF, a, off:CH],
                                     start=first, stop=last_one)
                last.then_inc(pv_done, 1)

            def two_slots(pair, s, jobs, base):
                now = [(i, e) for i, e in enumerate(jobs) if e[0] in (s, s + 1)]
                for i, e in now:
                    if e[1] == "den":
                        job(i, base, e, pair)
                for u in (s + LEAD, s + LEAD + 1):
                    if u < UNITS:
                        score(pair, u)
                    elif jobs is not LAST_JOBS:
                        score(pair + 1, u - UNITS)
                for i, e in now:
                    if e[1] != "den":
                        job(i, base, e, pair + 1 if e[3] else pair)
                for v in (s, s + 1):
                    attend(pair + v // UNITS, v % UNITS)

            def first_two_slots(s):
                for u in (s + LEAD, s + LEAD + 1):
                    score(0, u, score_needs(u), True)
                for i, e in enumerate(FIRST_JOBS):
                    if e[0] in (s, s + 1):
                        job(i, 0, e, 0, first=True)
                for v in (s, s + 1):
                    attend(0, v, after("V", UNITS_OF[v][1] // TPC), True)

            def after(kind, c):
                return 1 + next(i for i, e in enumerate(FIRST_JOBS) if e[1:3] == (kind, c))

            def score_needs(u):
                c, jt, _ = UNITS_OF[u]
                return max(after("K", jt // TPC), after("Q", c))

            for i, e in enumerate(FIRST_JOBS):
                if e[0] < 0:
                    job(i, 0, e, 0, first=True)
            for u in range(LEAD):
                score(0, u, score_needs(u), fresh=True)
            for s in range(0, ROT, 2):
                first_two_slots(s)
            with pe.Fori(0, PAIRS - 1) as p:
                for s in range(ROT, ROT + UNITS, 2):
                    two_slots(p, s, JOBS, p * NJ + NFJ)
            for s in range(ROT, UNITS, 2):
                two_slots(PAIRS - 1, s, LAST_JOBS, (PAIRS - 1) * NJ + NFJ)
            for i, e in enumerate(LAST_JOBS):
                if e[0] >= UNITS:
                    job(i, (PAIRS - 1) * NJ + NFJ, e, PAIRS - 1)

            ffn(1)

        @block.scalar
        def _(act):
            def roots(n):
                act.wait_ge(root_asked, n + 1)
                act.activation(root_out[:, :, :], root_in[:, :, :], ACT.Sqrt).then_inc(root_done, 1)

            def high_part(b, c):
                act.wait_ge(xn_turned, b + c + 1)
                if c >= 2:
                    act.wait_ge(up_done, FT * (b + c - 1))
                act.copy(xh[:, c % 2, :], psum[:, c % 2, :]).then_inc(xh_ready, 1)

            def ffn(k):
                b = CHUNKS * k
                high_part(b, 0)
                for c in range(CHUNKS):
                    if c + 1 < CHUNKS:
                        high_part(b, c + 1)
                    for f in range(FT):
                        act.wait_ge(up_done, FT * (b + c) + f + 1)
                        if c >= 2:
                            act.wait_ge(h_split, FT * (b + c - 2) + f + 1)
                            act.wait_ge(sq_done, FT * (b + c - 2) + f + 1)
                        act.activation(h[:, c % 2, f, :], psum[:, 2 + f, :], ACT.Gelu).then_inc(gelu_done, 1)
                    if c > 0:
                        store_y(b, c - 1)
                    for f in range(FT):
                        act.wait_ge(gelu_done, FT * (b + c) + f + 1)
                        if c >= 2 and f == 0:
                            act.wait_ge(ss_done, b + c - 1)
                        o = hsq[c % 2][:, f, :]
                        act.activation(o, h[:, c % 2, f, :], ACT.Square).then_inc(sq_done, 1)
                store_y(b, CHUNKS - 1)

            def store_y(b, c):
                act.wait_ge(down_done, b + c + 1)
                act.copy(yT[:, CH * c:CH * (c + 1)], Y_BANK).then_inc(yT_stored, 1)

            act.dma_start(w_up_nat[:, :, :], w_up.rearrange("(t p) d -> p t d", p=P)).then_inc(ffn_w_loaded, 16)
            act.dma_start(w_dn_nat[:, :], w_down).then_inc(ffn_w_loaded, 16)
            roots(0)
            ffn(0)
            roots(1)
            roots(2)

            def normalise_xa(r):
                act.wait_ge(scale_ready, 1)
                for t in range(TPC):
                    i = TPC * ORDER[r] + t
                    ins = act.activation(xn[:, r, t, :], X[:, i, :], ACT.Identity, bias=shift_t[:, i:i + 1],
                                         scale=scale_t[:, i:i + 1])
                ins.then_inc(xa_ready, 1)

            def store_xa(r):
                i = next(i for i, e in enumerate(FIRST_JOBS) if e[1:3] == ("xa", ORDER[r]))
                cols = slice(CH * ORDER[r], CH * (ORDER[r] + 1))
                act.wait_ge(side_done, i + 1)
                act.copy(xah[:, cols], side(i, True)).then_inc(xah_stored, 1)
                act.copy(xaT[:, cols], side(i, True)).then_inc(xaT_stored, 1)

            normalise_xa(0)
            normalise_xa(1)
            store_xa(0)
            normalise_xa(2)
            store_xa(1)
            normalise_xa(3)
            store_xa(2)

            def clamp(pair, u, fresh=False):
                c, jt, off = UNITS_OF[u]
                act.wait_ge(scored, pair * UNITS + u + 1)
                if not (fresh and u < 2):
                    act.wait_ge(exp_done, pair * UNITS + u - 1)
                act.activation(clamped[:, u % 2, :, off:CH], S(u % 2)[:, :, off:CH], ACT.Tanh,
                               scale=SCALE / SOFTCLAMP).then_inc(clamp_done, 1)

            def exps(pair, u, fresh=False):
                c, jt, off = UNITS_OF[u]
                act.wait_ge(clamp_done, pair * UNITS + u + 1)
                if not (fresh and u < PBUF):
                    act.wait_ge(pv_done, pair * UNITS + u + 1 - PBUF)
                    act.wait_ge(summed, pair * UNITS + u + 1 - PBUF)
                act.activation(probs[:, u % PBUF, :, off:CH], clamped[:, u % 2, :, off:CH], ACT.Exp,
                               scale=SOFTCLAMP).then_inc(exp_done, 1)

            def slot(pair, s, fresh=False, last=False):
                if s + 1 < UNITS:
                    clamp(pair, s + 1, fresh)
                elif not last:
                    clamp(pair + 1, s + 1 - UNITS)
                exps(pair + s // UNITS, s % UNITS, fresh)

            clamp(0, 0, True)
            for s in range(ROT):
                slot(0, s, True)
                if s == 2:
                    store_xa(3)
            with act.Fori(0, PAIRS - 1) as p:
                for s in range(ROT, ROT + UNITS):
                    slot(p, s)
            for s in range(ROT, UNITS):
                slot(PAIRS - 1, s, last=True)

            roots(3)
            ffn(1)
            roots(4)

        @block.gpsimd
        def _(pool):
            pool.memset(ones[:, :], 1.0).then_inc(consts_ready, 1)
            pool.memset(ident[:, :], 0.0).then_inc(consts_ready, 1)
            pool.wait_ge(consts_ready, 2)
            pool.affine_select(out=ident[:, :], in_=ident[:, :], pattern=[[-1, P]], compare_op=ALU.not_equal,
                               fill=1.0, base=0, channel_multiplier=1).then_inc(consts_ready, 1)
            pool.memset(causal[:, :, :], 1.0).then_inc(consts_ready, 1)
            pool.wait_ge(consts_ready, 4)
            pool.affine_select(out=causal[:, :, :], in_=causal[:, :, :], pattern=[[0, 2], [1, P]],
                               compare_op=ALU.is_ge, fill=0.0, base=0, channel_multiplier=-1).then_inc(consts_ready, 1)
            pool.wait_ge(consts_ready, 5)

            def sum_squares(k):
                for c in range(CHUNKS):
                    n = CHUNKS * k + c
                    sq = hsq[c % 2]
                    pool.wait_ge(sq_done, FT * (n + 1))
                    pool.tensor_tensor(sq[:, 0, :], sq[:, 0, :], sq[:, 1, :], ALU.add).then_inc(gstep, 1)
                    pool.tensor_tensor(sq[:, 2, :], sq[:, 2, :], sq[:, 3, :], ALU.add).then_inc(gstep, 1)
                    pool.wait_ge(gstep, 3 * n + 2)
                    pool.tensor_tensor(sq[:, 0, :], sq[:, 0, :], sq[:, 2, :], ALU.add).then_inc(gstep, 1)

            def mask(pair, u):
                c, jt, off = UNITS_OF[u]
                pool.wait_ge(exp_done, pair * UNITS + u + 1)
                tile = probs[:, u % PBUF, :, off:off + P]
                pool.tensor_tensor(tile, tile, causal[:, :, :], ALU.mult).then_inc(masked, 1)

            def add_probs(pair, u):
                c = UNITS_OF[u][0]
                pool.wait_ge(exp_done, pair * UNITS + u + 1)
                pool.wait_ge(summed, pair * UNITS + u)
                total = psums[:, rank[c] % 2, :, :]
                pool.tensor_tensor(total, total, probs[:, u % PBUF, :, :], ALU.add).then_inc(summed, 1)

            sum_squares(0)
            def slot(pair, u):
                if u in diag_rank:
                    mask(pair, u)
                if u in POOL_SUMS:
                    add_probs(pair, u)

            for s in range(ROT):
                slot(0, s)
            with pool.Fori(0, PAIRS - 1) as p:
                for s in range(ROT, ROT + UNITS):
                    slot(p + s // UNITS, s % UNITS)
            for s in range(ROT, UNITS):
                slot(PAIRS - 1, s)
            sum_squares(1)

        @block.vector
        def _(dve):
            steps = [0]

            def step(ins):
                steps[0] += 1
                ins.then_inc(vstep, 1)
                dve.wait_ge(vstep, steps[0])

            def ternary():
                dve.wait_ge(ffn_w_loaded, 32)
                w_up_flat = w_up_nat[:, :, :].rearrange("p t d -> p (t d)")
                for i, w in enumerate((w_up_flat, w_dn_nat[:, :])):
                    dve.scalar_tensor_tensor(tern_neg[:, :], w, -1.0, w, ALU.mult, ALU.max).then_inc(abs_summed, 1)
                    dve.wait_ge(abs_summed, 2 * i + 1)
                    dve.tensor_reduce(abs_sum[:, i:i + 1], tern_neg[:, :], mybir.AxisListType.X,
                                      ALU.add).then_inc(abs_summed, 1)
                    dve.wait_ge(abs_summed, 2 * i + 2)
                dve.wait_ge(thr_summed, 1)
                dve.tensor_scalar(thr[:, 0:2], SS_BANK[:, 0:2], 0.5 / (F * D), None, ALU.mult)
                step(dve.tensor_scalar(thr[:, 2:4], SS_BANK[:, 0:2], -0.5 / (F * D), None, ALU.mult))
                for i, w in enumerate((w_up_flat, w_dn_nat[:, :])):
                    step(dve.tensor_scalar(tern_neg[:, :], w, thr[:, 2 + i:3 + i], None, ALU.is_lt))
                    dve.scalar_tensor_tensor(w, w, thr[:, i:i + 1], tern_neg[:, :], ALU.is_gt,
                                             ALU.subtract).then_inc(tern_ready, 1)
                    dve.wait_ge(tern_ready, i + 1)
                dve.wait_ge(tern_turned, 1)
                dve.tensor_copy(w_up_t[:, :], psum[:, 0, :]).then_inc(tern_stored, 1)
                dve.tensor_copy(w_dn_t[:, :, :].rearrange("p t d -> p (t d)"), psum[:, 1, :]).then_inc(tern_stored, 1)
                dve.memset(yT[:, :], 0.0).then_inc(yT_cleared, 1)

            def statistics(c):
                for t in range(TPC * c, TPC * (c + 1)):
                    ins = dve.bn_stats(stats[:, t, :], X[:, t, :])
                step(ins)
                for t in range(TPC * c, TPC * (c + 1)):
                    ins = dve.bn_aggr(mv[:, t, :], stats[:, t, :])
                step(ins)

            def norm_scale(n, with_rms):
                step(dve.tensor_scalar(root_in[:, 0, :], mv[:, :, 1], LN_EPS, None, ALU.add))
                if with_rms:
                    step(dve.reciprocal(small[:, :], root_in[:, 0, :]))
                    ins = dve.tensor_tensor(root_in[:, 1, :], small[:, :], mv[:, :, 1], ALU.mult)
                else:
                    ins = dve.tensor_copy(root_in[:, 1, :], root_in[:, 0, :])
                ins.then_inc(root_asked, 1)
                if n == 0:
                    ternary()
                dve.wait_ge(root_done, n + 1)
                if with_rms:
                    step(dve.scalar_tensor_tensor(small[:, :], root_out[:, 1, :], RMS_EPS, root_out[:, 0, :],
                                                  ALU.add, ALU.mult))
                    step(dve.reciprocal(scale_t[:, :], small[:, :]))
                else:
                    step(dve.reciprocal(scale_t[:, :], root_out[:, 0, :]))

            def normalise(n, c):
                if n >= 2:
                    dve.wait_ge(xn_turned, n - 1)
                for t in range(TPC):
                    i = TPC * c + t
                    ins = dve.tensor_scalar(xn[:, n % 2, t, :], X[:, i, :], mv[:, i, 0:1], scale_t[:, i:i + 1],
                                            ALU.subtract, ALU.mult)
                ins.then_inc(xn_ready, 1)

            def low_part(b, c):
                dve.wait_ge(xh_ready, b + c + 1)
                if c >= 2:
                    dve.wait_ge(up_done, FT * (b + c - 1))
                dve.tensor_tensor(xl[:, c % 2, :], psum[:, c % 2, :], xh[:, c % 2, :].bitcast(F32),
                                  ALU.subtract).then_inc(xl_ready, 1)

            def ffn(k, n_root):
                b = CHUNKS * k
                normalise(b, 0)
                normalise(b + 1, 1)
                low_part(b, 0)
                for c in range(CHUNKS):
                    if c + 1 < CHUNKS:
                        low_part(b, c + 1)
                    if c + 2 < CHUNKS:
                        normalise(b + c + 2, c + 2)
                    if c > 0:
                        dve.wait_ge(down_done, b + c)
                    for f in range(FT):
                        dve.wait_ge(gelu_done, FT * (b + c) + f + 1)
                        step(dve.tensor_copy(hh[c % 2][:, f, :], h[:, c % 2, f, :]))
                        dve.tensor_tensor(hl[c % 2][:, f, :], h[:, c % 2, f, :], hh[c % 2][:, f, :].bitcast(F32),
                                          ALU.subtract).then_inc(h_split, 1)
                dve.wait_ge(ss_done, b + CHUNKS)
                dve.tensor_scalar(root_in[:, 0, :], SS_BANK[:, 0:TILES], 1.0 / F, None,
                                  ALU.mult).then_inc(root_asked, 1)
                dve.wait_ge(root_done, n_root + 1)
                step(dve.tensor_scalar(small[:, :], root_out[:, 0, :], RMS_EPS, 2.0, ALU.add, ALU.mult))
                step(dve.reciprocal(scale_t[:, :], small[:, :]))
                for r, c in enumerate(ORDER):
                    dve.wait_ge(y_turned, b + r + 1)
                    for t in range(TPC):
                        i = TPC * c + t
                        ins = dve.scalar_tensor_tensor(X[:, i, :], psum[:, r % 2, P * t:P * (t + 1)],
                                                       scale_t[:, i:i + 1], X[:, i, :], ALU.mult, ALU.add)
                    ins.then_inc(x_updated, 1)
                    if k == 0:
                        dve.wait_ge(x_updated, r + 1)
                        statistics(c)

            for c in range(CHUNKS):
                dve.wait_ge(x_loaded[c], 16)
                statistics(c)
            norm_scale(0, True)
            ffn(0, 1)
            norm_scale(2, False)
            dve.wait_ge(vstep, steps[0])
            dve.scalar_tensor_tensor(shift_t[:, :], mv[:, :, 0], -1.0, scale_t[:, :], ALU.mult,
                                     ALU.mult).then_inc(scale_ready, 1)
            dve.memset(yT[:, :], 0.0).then_inc(yT_cleared, 1)

            def split(bank, c, T, chain):
                cols = slice(CH * c, CH * (c + 1))
                lo, hi = slice(0, DH), slice(DH, P)
                dve.tensor_copy(T[lo, 0, cols], bank[lo, :])
                dve.tensor_copy(T[hi, 1, cols], bank[hi, :]).then_inc(vchain, 1)
                dve.wait_ge(vchain, chain + 1)
                dve.tensor_tensor(T[hi, 0, cols], bank[lo, :], T[lo, 0, cols].bitcast(F32), ALU.subtract)
                return dve.tensor_tensor(T[lo, 1, cols], bank[hi, :], T[hi, 1, cols].bitcast(F32), ALU.subtract)

            def last_use(pair, units):
                return (pair - 1) * UNITS + units

            def take(i, base, entry, pair, chain, first=False):
                _, kind, c, _ = entry
                bank = side(i, first)
                cols = slice(CH * c, CH * (c + 1))
                dve.wait_ge(side_done, base + i + 1)
                if kind == "K":
                    if not first:
                        dve.wait_ge(scored, last_use(pair, first_unit[c] + TPC))
                    split(bank, c, K1, chain).then_inc(side_taken, 1)
                elif kind == "Q":
                    if not first:
                        dve.wait_ge(scored, last_use(pair, last_unit[c] + 1))
                    split(bank, c, Qs, chain).then_inc(side_taken, 1)
                elif kind == "V":
                    if not first:
                        dve.wait_ge(pv_done, last_use(pair, first_unit[c] + TPC))
                    dve.tensor_copy(V[:, TPC * c:TPC * (c + 1), :].rearrange("p t f -> p (t f)"),
                                    bank).then_inc(side_taken, 1)
                elif kind == "WT":
                    qk = bank[:, 0:2 * P].rearrange("p (i f) -> p i f", i=2)
                    dve.tensor_copy(WTh[:, :, :], qk).then_inc(vchain, 1)
                    dve.tensor_copy(WvT[:, :], bank[:, 2 * P:3 * P])
                    dve.wait_ge(vchain, chain + 1)
                    dve.tensor_tensor(WTl[:, :, :], qk, WTh[:, :, :].bitcast(F32), ALU.subtract).then_inc(side_taken, 1)
                elif kind == "xa":
                    dve.wait_ge(xah_stored, rank[c] + 1)
                    dve.wait_ge(xaT_stored, rank[c] + 1)
                    dve.tensor_tensor(xal[:, cols], bank, xah[:, cols].bitcast(F32), ALU.subtract).then_inc(side_taken, 1)
                elif kind == "fin":
                    x_c = X[:, TPC * c:TPC * (c + 1), :].rearrange("p t d -> p (t d)")
                    dve.tensor_tensor(x_c, bank, x_c, ALU.add).then_inc(side_taken, 1)
                    dve.wait_ge(side_taken, base + i + 1)
                    statistics(c)
                elif kind == "WoT":
                    dve.tensor_copy(WoT[:, :], bank[:, 0:P]).then_inc(side_taken, 1)
                elif kind == "den":
                    dve.transpose(den_t[:, :], bank).then_inc(side_taken, 1)
                    dve.wait_ge(side_taken, base + i + 1)
                    own = den_t[:, :].rearrange("p (b k) -> p b k", k=32)
                    dve.reciprocal(den_r[:, :], own[:, :, 0]).then_inc(vchain, 1)
                    dve.wait_ge(vchain, chain + 1)
                    dve.tensor_copy(den_b[:, :].rearrange("p (b k) -> p b k", k=32),
                                    den_r[:, :].unsqueeze(2).broadcast_to([P, CH // 32, 32])).then_inc(vchain, 1)
                    dve.wait_ge(vchain, chain + 2)
                    dve.transpose(rden[:, :], den_b[:, :]).then_inc(vchain, 1)
                    dve.wait_ge(vchain, chain + 3)
                    dve.wait_ge(pv_done, pair * UNITS + last_unit[c] + 1)
                    dve.tensor_tensor(OT[:, rank[c] % 2, :], O(rank[c]), rden[:, :], ALU.mult).then_inc(normed, 1)
                elif kind == "out":
                    dve.tensor_tensor(yT[:, cols], bank, yT[:, cols], ALU.add).then_inc(side_taken, 1)

            def add_probs(pair, u):
                c, jt, off = UNITS_OF[u]
                if u in POOL_SUMS:
                    return
                if u in diag_rank:
                    dve.wait_ge(masked, pair * DIAGS + diag_rank[u])
                else:
                    dve.wait_ge(exp_done, pair * UNITS + u + 1)
                dve.wait_ge(summed, pair * UNITS + u)
                total = psums[:, rank[c] % 2, :, off:CH]
                new = probs[:, u % PBUF, :, off:CH]
                if u == first_unit[c]:
                    dve.tensor_copy(total, new).then_inc(summed, 1)
                else:
                    dve.tensor_tensor(total, total, new, ALU.add).then_inc(summed, 1)

            def chain_before(jobs, i):
                return sum(CHAIN.get(e[1], 0) for e in jobs[:i])

            def slot(pair, s, jobs, base, chain):
                for i, e in enumerate(jobs):
                    if e[0] == s:
                        take(i, base, e, pair + 1 if e[3] else pair, chain + chain_before(jobs, i))
                u = s + AHEAD
                if u < UNITS:
                    add_probs(pair, u)
                elif jobs is not LAST_JOBS:
                    add_probs(pair + 1, u - UNITS)

            for s in range(-1, ROT):
                for i, e in enumerate(FIRST_JOBS):
                    if e[0] == s:
                        take(i, 0, e, 0, chain_before(FIRST_JOBS, i), first=True)
                if s == -1:
                    for u in range(AHEAD):
                        add_probs(0, u)
                else:
                    add_probs(0, s + AHEAD)
            with dve.Fori(0, PAIRS - 1) as p:
                for s in range(ROT, ROT + UNITS):
                    slot(p, s, JOBS, p * NJ + NFJ, p * NC + NFC)
            for s in range(ROT, UNITS + ROT):
                slot(PAIRS - 1, s, LAST_JOBS, (PAIRS - 1) * NJ + NFJ, (PAIRS - 1) * NC + NFC)

            norm_scale(3, True)
            ffn(1, 4)


_INS = ["L0_attn_x", "L0_attn_Wq", "L0_attn_Wk", "L0_attn_Wv", "L0_attn_Wo", "L0_ffn_w_up", "L0_ffn_w_down"]


def kernel(**inputs):
    import numpy as _np
    import concourse.bacc as _bacc
    from concourse import mybir as _mybir
    from concourse.bass_utils import run_bass_kernel_spmd as _run

    nc = _bacc.Bacc("TRN2", target_bir_lowering=False, num_devices=1)
    arrays, args = {}, []
    for name in _INS:
        a = _np.ascontiguousarray(inputs[name])
        arrays[f"in_{name}_dram"] = a
        args.append(nc.dram_tensor(f"in_{name}_dram", a.shape, _mybir.dt.from_np(a.dtype), kind="ExternalInput").ap())
    shape = tuple(inputs["L0_attn_x"].shape)
    args.append(nc.dram_tensor("out_0_dram", shape, _mybir.dt.float32, kind="ExternalOutput").ap())
    bass_macaron_block(nc, *args)
    r = _run(nc, [arrays], core_ids=[0])
    return r.results[0]["out_0_dram"]
```

```python
from contextlib import ExitStack

import concourse.bass as bass
from concourse import mybir

ALU = mybir.AluOpType
ACT = mybir.ActivationFunctionType
F32 = mybir.dt.float32
F32R = mybir.dt.float32r

P = 128
CH = 512
TPC = CH // P
LEAD = 4
AHEAD = 2
PBUF = 5
ROT = 14


def causal_units(chunks):
    units = []
    for c in reversed(range(chunks)):
        units += [(c, TPC * c + k, P * k) for k in range(TPC)]
        units += [(c, jt, 0) for jt in reversed(range(TPC * c))]
    return units


def bass_macaron_block(nc: bass.Bass, x, wq, wk, wv, wo, w_up, w_down, out):
    _, N, D = x.shape
    F = w_up.shape[0]
    HDH = wq.shape[0]
    DH = 64
    PAIRS = HDH // P
    TILES = N // P
    CHUNKS = N // CH
    FT = F // P
    LN_EPS, RMS_EPS = 1e-5, 1e-8
    SOFTCLAMP = 50.0
    SCALE = DH ** -0.5
    assert D == P and N % CH == 0 and HDH % P == 0 and P == 2 * DH and F % P == 0 and CHUNKS == 4

    UNITS_OF = causal_units(CHUNKS)
    UNITS = len(UNITS_OF)
    first_unit = {c: min(u for u in range(UNITS) if UNITS_OF[u][0] == c) for c in range(CHUNKS)}
    last_unit = {c: max(u for u in range(UNITS) if UNITS_OF[u][0] == c) for c in range(CHUNKS)}
    rank = {c: CHUNKS - 1 - c for c in range(CHUNKS)}
    diag_rank = {}
    for u, (c, jt, _) in enumerate(UNITS_OF):
        if jt >= TPC * c:
            diag_rank[u] = len(diag_rank) + 1
    DIAGS = len(diag_rank)
    POOL_SUMS = (8, 11, 14, 22, 25, 33)

    JOBS = [
        (15, "WT", 0, 1), (16, "WoT", 0, 0), (17, "K", 3, 1), (18, "den", 3, 0), (19, "V", 3, 1), (21, "out", 3, 0),
        (22, "Q", 3, 1), (24, "K", 2, 1), (26, "V", 2, 1), (30, "den", 2, 0), (31, "K", 1, 1), (33, "out", 2, 0),
        (34, "V", 1, 1), (35, "Q", 2, 1), (37, "Q", 1, 1), (38, "den", 1, 0), (40, "den", 0, 0), (41, "K", 0, 1),
        (43, "out", 1, 0), (45, "V", 0, 1), (46, "out", 0, 0), (50, "Q", 0, 1),
    ]
    FIRST_JOBS = [(-1, "WT", 0, 0), (-1, "xa", 3, 0), (-1, "xa", 2, 0), (-1, "K", 3, 0), (-1, "Q", 3, 0),
                  (-1, "K", 2, 0), (-1, "xa", 1, 0), (-1, "V", 3, 0), (-1, "K", 1, 0), (0, "xa", 0, 0),
                  (2, "V", 2, 0), (3, "K", 0, 0), (6, "V", 1, 0), (9, "Q", 2, 0), (10, "V", 0, 0), (12, "Q", 1, 0),
                  (13, "Q", 0, 0)]
    LAST_JOBS = [(16, "WoT", 0, 0), (18, "den", 3, 0), (21, "out", 3, 0), (24, "fin", 3, 0), (30, "den", 2, 0),
                 (33, "out", 2, 0), (34, "fin", 2, 0), (38, "den", 1, 0), (UNITS, "den", 0, 0), (UNITS, "out", 1, 0),
                 (UNITS, "fin", 1, 0), (UNITS, "out", 0, 0), (UNITS, "fin", 0, 0)]
    WT_JOB, XA3_JOB, XA2_JOB, XA1_JOB = 0, 1, 2, 6
    ORDER = list(reversed(range(CHUNKS)))
    CHAIN = {"K": 1, "Q": 1, "WT": 1, "den": 3}
    SCALAR_HIGH = [i for i, e in enumerate(FIRST_JOBS) if e[1:3] in (("K", 3), ("Q", 3), ("K", 2))]
    NJ, NFJ = len(JOBS), len(FIRST_JOBS)

    def chain_before(jobs, i):
        return sum(CHAIN.get(e[1], 0) for n, e in enumerate(jobs[:i]) if jobs is not FIRST_JOBS or n not in SCALAR_HIGH)

    NC, NFC = chain_before(JOBS, NJ), chain_before(FIRST_JOBS, NFJ)
    assert NJ % 2 == 0 and JOBS == sorted(JOBS, key=lambda e: e[0]) and ROT % 2 == UNITS % 2 == UNITS % PBUF == 0

    with ExitStack() as ctx:
        def sb(name, shape, dt=F32):
            return ctx.enter_context(nc.sbuf_tensor(name, shape, dt))

        def sem(name):
            return ctx.enter_context(nc.semaphore(name))

        psum = ctx.enter_context(nc.psum_tensor("psum", [P, 8, CH], F32))

        ident = sb("ident", [P, P])
        ones = sb("ones", [P, P])
        causal = sb("causal", [P, 2, P])
        X = sb("X", [P, TILES, D])
        w_up_nat = sb("w_up_nat", [P, FT, D])
        w_dn_nat = sb("w_dn_nat", [P, F])
        tern_neg = sb("tern_neg", [P, 2, F])
        w_up_t = sb("w_up_t", [P, F], F32R)
        w_dn_t = sb("w_dn_t", [P, FT, D], F32R)
        abs_sum = sb("abs_sum", [P, 2])
        thr = sb("thr", [P, 4])
        stats = sb("stats", [P, TILES, 6])
        mv = sb("mv", [P, TILES, 2])
        root_in = sb("root_in", [P, 2, TILES])
        root_out = sb("root_out", [P, 2, TILES])
        small = sb("small", [P, TILES])
        scale_t = sb("scale_t", [P, TILES])
        shift_t = sb("shift_t", [P, TILES])
        xn = sb("xn", [P, 4, TPC, D])
        xaT = sb("xaT", [P, N])
        yT = sb("yT", [P, N])

        Qs = sb("Qs", [P, 2, N], F32R)
        K1 = sb("K1", [P, 2, N], F32R)
        K2 = sb("K2", [P, 2, N], F32R)
        V = sb("V", [P, TILES, P])
        clamped = sb("clamped", [P, 2, 2, CH])
        probs = sb("probs", [P, PBUF, 2, CH])
        psums = sb("psums", [P, 2, 2, CH])
        den_t = sb("den_t", [P, CH])
        den_r = sb("den_r", [P, CH // 32])
        den_b = sb("den_b", [P, CH])
        rden = sb("rden", [P, CH])
        OT = sb("OT", [P, 2, CH])
        raw_qkv = sb("raw_qkv", [P, 3, D])
        raw_o = sb("raw_o", [P, P])
        WTh = sb("WTh", [P, 2, P], F32R)
        WTl = sb("WTl", [P, 2, P], F32R)
        WvT = sb("WvT", [P, P])
        xah = sb("xah", [P, N], F32R)
        xal = sb("xal", [P, N], F32R)
        WoT = sb("WoT", [P, D])

        xh = K1[:, 0, 0:2 * CH].rearrange("p (b n) -> p b n", b=2)
        xl = K1[:, 1, 0:2 * CH].rearrange("p (b n) -> p b n", b=2)
        hh, hl = ([T[:, part, :].rearrange("p (f n) -> p f n", f=FT) for T in (Qs, K2)] for part in range(2))
        h = probs[:, 0:4, :, :].rearrange("p a b n -> p (a b) n").rearrange("p (b f) n -> p b f n", b=2)
        hsq = [clamped[:, :, :, :].rearrange("p a b n -> p (a b) n"), psums[:, :, :, :].rearrange("p a b n -> p (a b) n")]

        consts_ready = sem("consts_ready")
        x_loaded = [sem(f"x_loaded{c}") for c in range(CHUNKS)]
        w_up_loaded = sem("w_up_loaded")
        w_dn_loaded = sem("w_dn_loaded")
        vstep = sem("vstep")
        last_sq_summed = sem("last_sq_summed")
        gstep = sem("gstep")
        abs_summed = sem("abs_summed")
        thr_summed = sem("thr_summed")
        tern_up_ready = sem("tern_up_ready")
        tern_dn_ready = sem("tern_dn_ready")
        tern_turned = sem("tern_turned")
        tern_stored = sem("tern_stored")
        root_asked = sem("root_asked")
        root_done = sem("root_done")
        xn_ready = sem("xn_ready")
        xn_turned = sem("xn_turned")
        xh_ready = sem("xh_ready")
        xl_ready = sem("xl_ready")
        up_done = sem("up_done")
        gelu_done = sem("gelu_done")
        sq_done = sem("sq_done")
        h_split = sem("h_split")
        down_done = sem("down_done")
        ss_done = sem("ss_done")
        yT_stored = sem("yT_stored")
        y_turned = sem("y_turned")
        x_updated = sem("x_updated")
        yT_cleared = sem("yT_cleared")
        thr_ready = sem("thr_ready")
        dn_step = sem("dn_step")
        scale_ready = sem("scale_ready")
        xa_ready = sem("xa_ready")
        xah_stored = sem("xah_stored")
        xaT_stored = sem("xaT_stored")
        raw_loaded = sem("raw_loaded")
        raw_o_loaded = sem("raw_o_loaded")
        side_done = sem("side_done")
        side_taken = sem("side_taken")
        high_copied = sem("high_copied")
        vchain = sem("vchain")
        k_swapped = sem("k_swapped")
        scored = sem("scored")
        clamp_done = sem("clamp_done")
        exp_done = sem("exp_done")
        masked = sem("masked")
        summed = sem("summed")
        pv_done = sem("pv_done")
        normed = sem("normed")
        out_stored = sem("out_stored")

        x_v = x[0].rearrange("(t p) d -> p t d", p=P)
        out_v = out[0].rearrange("(t p) d -> p t d", p=P)
        wqkv_rows = [w.rearrange("(a p) d -> a p d", p=P) for w in (wq, wk, wv)]
        wo_cols = wo.rearrange("d (a f) -> a d f", f=P)

        def S(slot):
            return psum[:, 2 * slot:2 * slot + 2, :]

        def O(q):
            return psum[:, 4 + q % 2, :]

        def side(i, first=False):
            return psum[:, 6 + (i if first else i + NFJ) % 2, :]

        UP_BANKS = [[1, 2, 3, 6] * CHUNKS, [1, 2, 3, 1] + [2, 3, 1, 6] + [2, 3, 1, 6] * (CHUNKS - 2)]

        def UP(k, r, f):
            return psum[:, UP_BANKS[k][FT * r + f], :]

        def up_before(k, r, f):
            m = FT * r + f
            return max([i + 1 for i in range(m) if UP_BANKS[k][i] == UP_BANKS[k][m]], default=0)

        TURN_BANK, Y_BANK, SS_BANK = psum[:, 0, :], psum[:, 4, :], psum[:, 5, :]
        ALL_UNITS, ALL_NORMED = PAIRS * UNITS, PAIRS * CHUNKS

        def tiles_of(r):
            return slice(TPC * ORDER[r], TPC * (ORDER[r] + 1))

        def last_job(kind, c):
            return (PAIRS - 1) * NJ + NFJ + 1 + next(i for i, e in enumerate(LAST_JOBS) if e[1:3] == (kind, c))

        block = ctx.enter_context(nc.Block())

        @block.sync
        def _(sp):
            for c in ORDER:
                sp.dma_start(X[:, TPC * c:TPC * (c + 1), :], x_v[:, TPC * c:TPC * (c + 1), :]).then_inc(x_loaded[c], 16)

            def load_qkv(pair):
                for i, w in enumerate(wqkv_rows):
                    sp.dma_start(raw_qkv[:, i, :], w[pair]).then_inc(raw_loaded, 16)

            def swap_k(pair, c, taken):
                sp.wait_ge(side_taken, taken)
                sp.wait_ge(k_swapped, (pair * CHUNKS + rank[c]) * 32)
                cols = slice(CH * c, CH * (c + 1))
                sp.dma_start(K2[DH:P, :, cols].bitcast(F32), K1[0:DH, :, cols].bitcast(F32)).then_inc(k_swapped, 16)
                sp.dma_start(K2[0:DH, :, cols].bitcast(F32), K1[DH:P, :, cols].bitcast(F32)).then_inc(k_swapped, 16)

            load_qkv(0)
            sp.dma_start(raw_o[:, :], wo_cols[0]).then_inc(raw_o_loaded, 16)
            for i, (_, kind, c, _) in enumerate(FIRST_JOBS):
                if kind == "K":
                    swap_k(0, c, i + 1)

            with sp.Fori(0, PAIRS - 1) as p:
                load_qkv(p + 1)
                for i, (_, kind, c, _) in enumerate(JOBS):
                    if kind == "K":
                        swap_k(p + 1, c, p * NJ + NFJ + i + 1)
                    if kind == "WoT":
                        sp.wait_ge(side_taken, p * NJ + NFJ + i + 1)
                        sp.dma_start(raw_o[:, :], wo_cols[p + 1]).then_inc(raw_o_loaded, 16)

            for r, c in enumerate(ORDER):
                sp.wait_ge(x_updated, CHUNKS + 1 + r)
                sp.dma_start(out_v[:, TPC * c:TPC * (c + 1), :], X[:, TPC * c:TPC * (c + 1), :]).then_inc(out_stored, 16)
            sp.wait_ge(out_stored, 16 * CHUNKS)

        @block.tensor
        def _(pe):
            pe.wait_ge(consts_ready, 3)
            pe.wait_ge(abs_summed, 2)
            pe.matmul(SS_BANK[:, 0:2], ones[:, :], abs_sum[:, :], start=True, stop=True).then_inc(thr_summed, 1)
            pe.wait_ge(tern_up_ready, 1)
            for f in range(FT):
                last = pe.transpose(psum[:, 6, P * f:P * (f + 1)], w_up_nat[:, f, :], ident[:, :])
            last.then_inc(tern_turned, 1)

            def turn_xn(k, r):
                n = CHUNKS * k + r
                pe.wait_ge(xn_ready, n + 1)
                if r > 0:
                    pe.wait_ge(xl_ready, n)
                elif k == 1:
                    pe.wait_ge(clamp_done, ALL_UNITS)
                for t in range(TPC):
                    last = pe.transpose(TURN_BANK[:, P * t:P * (t + 1)], xn[:, n % 2, t, :], ident[:, :])
                last.then_inc(xn_turned, 1)

            def up(k, r):
                n = CHUNKS * k + r
                pe.wait_ge(xh_ready, n + 1)
                pe.wait_ge(xl_ready, n + 1)
                for f in range(FT):
                    if up_before(k, r, f) > 0:
                        pe.wait_ge(gelu_done, FT * CHUNKS * k + up_before(k, r, f))
                    elif k == 1 and UP_BANKS[k][FT * r + f] == 6:
                        pe.wait_ge(side_taken, last_job("out", 0))
                    w = w_up_t[:, P * f:P * (f + 1)]
                    pe.matmul(UP(k, r, f), w, xh[:, r % 2, :], start=True, stop=False)
                    pe.matmul(UP(k, r, f), w, xl[:, r % 2, :], start=False, stop=True).then_inc(up_done, 1)

            def down(k, r):
                n = CHUNKS * k + r
                if r > 0:
                    pe.wait_ge(yT_stored, n)
                elif k == 1:
                    pe.wait_ge(normed, ALL_NORMED - 1)
                for f in range(FT):
                    pe.wait_ge(h_split, FT * n + f + 1)
                    w = w_dn_t[:, f, :]
                    pe.matmul(Y_BANK, w, hh[r % 2][:, f, :], start=(f == 0), stop=False)
                    last = pe.matmul(Y_BANK, w, hl[r % 2][:, f, :], start=False, stop=(f == FT - 1))
                last.then_inc(down_done, 1)

            def sum_h(k, r):
                n = CHUNKS * k + r
                if r == CHUNKS - 1:
                    pe.wait_ge(last_sq_summed, k + 1)
                else:
                    pe.wait_ge(gstep, 3 * ((CHUNKS - 1) * k + r + 1))
                if k == 1 and r == 0:
                    pe.wait_ge(normed, ALL_NORMED)
                for t in range(TPC):
                    i = TPC * ORDER[r] + t
                    last = pe.matmul(SS_BANK[:, i:i + 1], hsq[r % 2][:, 0, P * t:P * (t + 1)], ones[:, 0:1],
                                     start=True, stop=True)
                last.then_inc(ss_done, 1)

            def turn_y(k, r):
                pe.wait_ge(yT_stored, CHUNKS * k + r + 1)
                turn_tokens(psum[:, r, :], ORDER[r]).then_inc(y_turned, 1)

            def turn_tokens(bank, c):
                for t in range(TPC):
                    last = pe.transpose(bank[:, P * t:P * (t + 1)],
                                        yT[:, CH * c + P * t:CH * c + P * (t + 1)], ident[:, :])
                return last

            turn_xn(0, 0)
            pe.wait_ge(tern_dn_ready, 1)
            for f in range(FT):
                last = pe.transpose(psum[:, 7, P * f:P * (f + 1)], w_dn_nat[:, P * f:P * (f + 1)], ident[:, :])
            last.then_inc(tern_turned, 1)
            pe.wait_ge(tern_stored, 2)
            turn_xn(0, 1)
            up(0, 0)
            turn_xn(0, 2)
            up(0, 1)
            down(0, 0)
            turn_xn(0, 3)
            up(0, 2)
            down(0, 1)
            sum_h(0, 0)
            up(0, 3)
            down(0, 2)
            sum_h(0, 1)

            def job(i_in, base, entry, pair, first=False):
                _, kind, c, _ = entry
                bank = side(i_in, first)
                cols = slice(CH * c, CH * (c + 1))
                if not first:
                    pe.wait_ge(side_taken, base + i_in - 1)
                elif i_in > 1:
                    pe.wait_ge(side_taken, i_in - 1)
                if kind in "KQ":
                    w = slice("QK".index(kind), "QK".index(kind) + 1)
                    pe.matmul(bank, WTh[:, w, :], xah[:, cols], start=True, stop=False)
                    pe.matmul(bank, WTh[:, w, :], xal[:, cols], start=False, stop=False)
                    last = pe.matmul(bank, WTl[:, w, :], xah[:, cols], start=False, stop=True)
                elif kind == "V":
                    for t in range(TPC):
                        a = CH * c + P * t
                        last = pe.matmul(bank[:, P * t:P * (t + 1)], xaT[:, a:a + P], WvT[:, :],
                                         start=True, stop=True)
                elif kind == "WT":
                    pe.wait_ge(raw_loaded, (pair + 1) * 48)
                    for i in range(3):
                        last = pe.transpose(bank[:, P * i:P * (i + 1)], raw_qkv[:, i, :], ident[:, :])
                elif kind == "WoT":
                    pe.wait_ge(raw_o_loaded, (pair + 1) * 16)
                    last = pe.transpose(bank[:, 0:P], raw_o[:, :], ident[:, :])
                elif kind == "xa":
                    pe.wait_ge(xa_ready, rank[c] + 1)
                    for t in range(TPC):
                        last = pe.transpose(bank[:, P * t:P * (t + 1)], xn[:, rank[c], t, :], ident[:, :])
                elif kind == "fin":
                    out_i = next(i for i, e in enumerate(LAST_JOBS) if e[1:3] == ("out", c))
                    pe.wait_ge(side_taken, base + out_i + 1)
                    last = turn_tokens(bank, c)
                elif kind == "den":
                    pe.wait_ge(summed, pair * UNITS + last_unit[c] + 1)
                    for a in range(2):
                        last = pe.matmul(bank[DH * a:DH * (a + 1), :], ones[:, 0:DH], psums[:, rank[c] % 2, a, :],
                                         start=True, stop=True)
                elif kind == "out":
                    pe.wait_ge(normed, pair * CHUNKS + rank[c] + 1)
                    last = pe.matmul(bank, WoT[:, :], OT[:, rank[c] % 2, :], start=True, stop=True)
                last.then_inc(side_done, 1)

            def first_use(jt, c):
                return jt % TPC == (0 if jt >= TPC * c else TPC - 1)

            def score(pair, u, need=None, fresh=False):
                c, jt, off = UNITS_OF[u]
                slot = u % 2
                if not (fresh and u < 2):
                    pe.wait_ge(clamp_done, pair * UNITS + u - 1)
                if need is not None:
                    pe.wait_ge(side_taken, need)
                if c == CHUNKS - 1 and first_use(jt, c):
                    pe.wait_ge(k_swapped, (pair * CHUNKS + rank[jt // TPC] + 1) * 32)
                for a in range(2):
                    o = S(slot)[:, a, off:CH]
                    q = Qs[:, a, CH * c + off:CH * (c + 1)]
                    pe.matmul(o, K1[:, a, P * jt:P * (jt + 1)], q, start=True, stop=False)
                    last = pe.matmul(o, K2[:, a, P * jt:P * (jt + 1)], q, start=False, stop=True)
                last.then_inc(scored, 1)

            def attend(pair, u, need=None, fresh=False):
                c, jt, off = UNITS_OF[u]
                first, last_one = u == first_unit[c], u == last_unit[c]
                if u in diag_rank:
                    pe.wait_ge(masked, pair * DIAGS + diag_rank[u])
                else:
                    pe.wait_ge(exp_done, pair * UNITS + u + 1)
                if first and not fresh and rank[c] != 1:
                    pe.wait_ge(normed, pair * CHUNKS + rank[c] - 1)
                if need is not None:
                    pe.wait_ge(side_taken, need)
                for a in ((0, 1), (1, 0))[u % 2]:
                    o = O(rank[c])[DH * a:DH * (a + 1), off:CH]
                    last = pe.matmul(o, V[:, jt, DH * a:DH * (a + 1)], probs[:, u % PBUF, a, off:CH],
                                     start=first, stop=last_one)
                last.then_inc(pv_done, 1)

            def two_slots(pair, s, jobs, base):
                now = [(i, e) for i, e in enumerate(jobs) if e[0] in (s, s + 1)]
                for i, e in now:
                    if e[1] == "den":
                        job(i, base, e, pair)
                for u in (s + LEAD, s + LEAD + 1):
                    if u < UNITS:
                        score(pair, u)
                    elif jobs is not LAST_JOBS:
                        score(pair + 1, u - UNITS)
                for i, e in now:
                    if e[1] != "den":
                        job(i, base, e, pair + 1 if e[3] else pair)
                for v in (s, s + 1):
                    attend(pair + v // UNITS, v % UNITS)

            def first_two_slots(s):
                for u in (s + LEAD, s + LEAD + 1):
                    score(0, u, score_needs(u), True)
                for i, e in enumerate(FIRST_JOBS):
                    if e[0] in (s, s + 1):
                        job(i, 0, e, 0, first=True)
                for v in (s, s + 1):
                    attend(0, v, after("V", UNITS_OF[v][1] // TPC), True)

            def after(kind, c):
                return 1 + next(i for i, e in enumerate(FIRST_JOBS) if e[1:3] == (kind, c))

            def score_needs(u):
                c, jt, _ = UNITS_OF[u]
                return max(after("K", jt // TPC), after("Q", c))

            pe.wait_ge(gelu_done, FT * CHUNKS)
            job(WT_JOB, 0, FIRST_JOBS[WT_JOB], 0, first=True)
            down(0, 3)
            sum_h(0, 2)
            sum_h(0, 3)
            for r in range(CHUNKS):
                turn_y(0, r)
            for i, e in enumerate(FIRST_JOBS):
                if i > WT_JOB and e[0] < 0:
                    job(i, 0, e, 0, first=True)
                if i == XA1_JOB:
                    for u in range(2):
                        score(0, u, score_needs(u), fresh=True)
            for u in range(2, LEAD):
                score(0, u, score_needs(u), fresh=True)
            for s in range(0, ROT, 2):
                first_two_slots(s)
            with pe.Fori(0, PAIRS - 1) as p:
                for s in range(ROT, ROT + UNITS, 2):
                    two_slots(p, s, JOBS, p * NJ + NFJ)
            for s in range(ROT, UNITS, 2):
                two_slots(PAIRS - 1, s, LAST_JOBS, (PAIRS - 1) * NJ + NFJ)

            def tail_job(kind, c):
                i = next(i for i, e in enumerate(LAST_JOBS) if e[1:3] == (kind, c))
                job(i, (PAIRS - 1) * NJ + NFJ, LAST_JOBS[i], PAIRS - 1)

            turn_xn(1, 0)
            tail_job("den", 0)
            tail_job("out", 1)
            up(1, 0)
            tail_job("fin", 1)
            tail_job("out", 0)
            turn_xn(1, 1)
            tail_job("fin", 0)
            up(1, 1)
            down(1, 0)
            turn_xn(1, 2)
            up(1, 2)
            turn_xn(1, 3)
            down(1, 1)
            sum_h(1, 0)
            up(1, 3)
            down(1, 2)
            sum_h(1, 1)
            down(1, 3)
            sum_h(1, 2)
            sum_h(1, 3)
            for r in range(CHUNKS):
                turn_y(1, r)

        @block.scalar
        def _(act):
            def roots(n, rows, tiles):
                act.wait_ge(root_asked, n + 1)
                act.activation(root_out[:, 0:rows, tiles], root_in[:, 0:rows, tiles], ACT.Sqrt).then_inc(root_done, 1)

            def high_part(k, r):
                n = CHUNKS * k + r
                act.wait_ge(xn_turned, n + 1)
                if r >= 2:
                    act.wait_ge(up_done, FT * (n - 1))
                elif k == 1:
                    act.wait_ge(scored, ALL_UNITS)
                act.copy(xh[:, r % 2, :], TURN_BANK).then_inc(xh_ready, 1)

            def gelus(k, r):
                n = CHUNKS * k + r
                for f in range(FT):
                    act.wait_ge(up_done, FT * n + f + 1)
                    if r >= 2:
                        act.wait_ge(h_split, FT * (n - 2) + f + 1)
                        act.wait_ge(sq_done, FT * (n - 2) + f + 1)
                    elif k == 1 and f == 0:
                        act.wait_ge(pv_done, ALL_UNITS)
                        act.wait_ge(summed, ALL_UNITS)
                    act.activation(h[:, r % 2, f, :], UP(k, r, f), ACT.Gelu).then_inc(gelu_done, 1)

            def squares(k, r):
                n = CHUNKS * k + r
                for f in range(FT):
                    act.wait_ge(gelu_done, FT * n + f + 1)
                    if f == 0 and r >= 2:
                        act.wait_ge(ss_done, n - 1)
                    elif f == 0 and k == 1:
                        act.wait_ge(*((exp_done, ALL_UNITS) if r == 0 else (side_done, last_job("den", 0))))
                    act.activation(hsq[r % 2][:, f, :], h[:, r % 2, f, :], ACT.Square).then_inc(sq_done, 1)

            def store_y(k, r):
                act.wait_ge(down_done, CHUNKS * k + r + 1)
                if k == 1:
                    act.wait_ge(side_done, last_job("fin", ORDER[r]))
                act.copy(yT[:, CH * ORDER[r]:CH * (ORDER[r] + 1)], Y_BANK).then_inc(yT_stored, 1)

            act.dma_start(w_up_nat[:, :, :], w_up.rearrange("(t p) d -> p t d", p=P)).then_inc(w_up_loaded, 16)
            act.dma_start(w_dn_nat[:, :], w_down).then_inc(w_dn_loaded, 16)
            act.wait_ge(w_up_loaded, 16)
            act.activation(hsq[0][:, 0, :], w_up_nat[:, :, :].rearrange("p t d -> p (t d)"), ACT.Abs,
                           accum_out=abs_sum[:, 0:1]).then_inc(abs_summed, 1)
            act.wait_ge(w_dn_loaded, 16)
            act.activation(hsq[0][:, 1, :], w_dn_nat[:, :], ACT.Abs,
                           accum_out=abs_sum[:, 1:2]).then_inc(abs_summed, 1)
            act.wait_ge(thr_summed, 1)
            act.mul(thr[:, 0:2], SS_BANK[:, 0:2], 0.5 / (F * D)).then_inc(thr_ready, 1)
            act.mul(thr[:, 2:4], SS_BANK[:, 0:2], -0.5 / (F * D)).then_inc(thr_ready, 1)
            roots(0, 2, slice(0, TILES))
            act.wait_ge(tern_turned, 1)
            act.copy(w_up_t[:, :], psum[:, 6, :]).then_inc(tern_stored, 1)
            high_part(0, 0)
            act.wait_ge(tern_turned, 2)
            act.copy(w_dn_t[:, :, :].rearrange("p t d -> p (t d)"), psum[:, 7, :]).then_inc(tern_stored, 1)
            high_part(0, 1)
            for r in range(CHUNKS):
                gelus(0, r)
                if r > 0:
                    store_y(0, r - 1)
                squares(0, r)
                if r + 2 < CHUNKS:
                    high_part(0, r + 2)
            store_y(0, CHUNKS - 1)
            roots(1, 1, slice(0, TILES))

            def normalise_xa(r):
                act.wait_ge(scale_ready, r + 1)
                for t in range(TPC):
                    i = TPC * ORDER[r] + t
                    ins = act.activation(xn[:, r, t, :], X[:, i, :], ACT.Identity, bias=shift_t[:, i:i + 1],
                                         scale=scale_t[:, i:i + 1])
                ins.then_inc(xa_ready, 1)

            def first_high(k):
                i = SCALAR_HIGH[k]
                T, c = (K1 if FIRST_JOBS[i][1] == "K" else Qs), FIRST_JOBS[i][2]
                cols = slice(CH * c, CH * (c + 1))
                act.wait_ge(side_done, i + 1)
                act.copy(T[0:DH, 0, cols], side(i, True)[0:DH, :])
                act.copy(T[DH:P, 1, cols], side(i, True)[DH:P, :]).then_inc(high_copied, 1)

            def store_xa(r):
                i = next(i for i, e in enumerate(FIRST_JOBS) if e[1:3] == ("xa", ORDER[r]))
                cols = slice(CH * ORDER[r], CH * (ORDER[r] + 1))
                act.wait_ge(side_done, i + 1)
                act.copy(xah[:, cols], side(i, True)).then_inc(xah_stored, 1)
                act.copy(xaT[:, cols], side(i, True)).then_inc(xaT_stored, 1)

            roots(2, 1, tiles_of(0))
            normalise_xa(0)
            roots(3, 1, tiles_of(1))
            normalise_xa(1)
            store_xa(0)
            roots(4, 1, tiles_of(2))
            normalise_xa(2)
            store_xa(1)
            roots(5, 1, tiles_of(3))
            first_high(0)
            normalise_xa(3)
            first_high(1)
            first_high(2)
            store_xa(2)

            def clamp(pair, u, fresh=False):
                c, jt, off = UNITS_OF[u]
                act.wait_ge(scored, pair * UNITS + u + 1)
                if not (fresh and u < 2):
                    act.wait_ge(exp_done, pair * UNITS + u - 1)
                act.activation(clamped[:, u % 2, :, off:CH], S(u % 2)[:, :, off:CH], ACT.Tanh,
                               scale=SCALE / SOFTCLAMP).then_inc(clamp_done, 1)

            def exps(pair, u, fresh=False):
                c, jt, off = UNITS_OF[u]
                act.wait_ge(clamp_done, pair * UNITS + u + 1)
                if not (fresh and u < PBUF):
                    act.wait_ge(pv_done, pair * UNITS + u + 1 - PBUF)
                    act.wait_ge(summed, pair * UNITS + u + 1 - PBUF)
                act.activation(probs[:, u % PBUF, :, off:CH], clamped[:, u % 2, :, off:CH], ACT.Exp,
                               scale=SOFTCLAMP).then_inc(exp_done, 1)

            def slot(pair, s, fresh=False, last=False):
                if s + 1 < UNITS:
                    clamp(pair, s + 1, fresh)
                elif not last:
                    clamp(pair + 1, s + 1 - UNITS)
                exps(pair + s // UNITS, s % UNITS, fresh)

            clamp(0, 0, True)
            for s in range(ROT):
                slot(0, s, True)
                if s == 2:
                    store_xa(3)
            with act.Fori(0, PAIRS - 1) as p:
                for s in range(ROT, ROT + UNITS):
                    slot(p, s)
            for s in range(ROT, UNITS):
                slot(PAIRS - 1, s, last=True)

            def normalise_first(r):
                act.wait_ge(scale_ready, CHUNKS + 1)
                for t in range(TPC):
                    i = TPC * ORDER[r] + t
                    ins = act.activation(xn[:, r, t, :], X[:, i, :], ACT.Identity, bias=shift_t[:, i:i + 1],
                                         scale=scale_t[:, i:i + 1])
                ins.then_inc(xn_ready, 1)

            roots(6, 2, slice(2 * TPC, TILES))
            normalise_first(0)
            high_part(1, 0)
            normalise_first(1)
            gelus(1, 0)
            high_part(1, 1)
            squares(1, 0)
            gelus(1, 1)
            roots(7, 2, slice(0, 2 * TPC))
            squares(1, 1)
            store_y(1, 0)
            high_part(1, 2)
            gelus(1, 2)
            high_part(1, 3)
            store_y(1, 1)
            squares(1, 2)
            gelus(1, 3)
            store_y(1, 2)
            squares(1, 3)
            store_y(1, 3)
            roots(8, 1, slice(0, TILES))

        @block.gpsimd
        def _(pool):
            pool.memset(ones[:, :], 1.0).then_inc(consts_ready, 1)
            pool.memset(ident[:, :], 0.0).then_inc(consts_ready, 1)
            pool.wait_ge(consts_ready, 2)
            pool.affine_select(out=ident[:, :], in_=ident[:, :], pattern=[[-1, P]], compare_op=ALU.not_equal,
                               fill=1.0, base=0, channel_multiplier=1).then_inc(consts_ready, 1)
            pool.memset(causal[:, :, :], 1.0).then_inc(consts_ready, 1)
            pool.wait_ge(consts_ready, 4)
            pool.affine_select(out=causal[:, :, :], in_=causal[:, :, :], pattern=[[0, 2], [1, P]],
                               compare_op=ALU.is_ge, fill=0.0, base=0, channel_multiplier=-1).then_inc(consts_ready, 1)
            pool.wait_ge(consts_ready, 5)

            w = w_dn_nat[:, :]
            pool.wait_ge(thr_ready, 2)
            pool.tensor_scalar(tern_neg[:, 1, :], w, thr[:, 3:4], None, ALU.is_lt).then_inc(dn_step, 1)
            pool.wait_ge(dn_step, 1)
            pool.tensor_scalar(w, w, thr[:, 1:2], None, ALU.is_gt).then_inc(dn_step, 1)
            pool.wait_ge(dn_step, 2)
            pool.tensor_tensor(w, w, tern_neg[:, 1, :], ALU.subtract).then_inc(tern_dn_ready, 1)

            def sum_squares(k):
                for r in range(CHUNKS - 1):
                    n = (CHUNKS - 1) * k + r
                    sq = hsq[r % 2]
                    pool.wait_ge(sq_done, FT * (CHUNKS * k + r + 1))
                    pool.tensor_tensor(sq[:, 0, :], sq[:, 0, :], sq[:, 1, :], ALU.add).then_inc(gstep, 1)
                    pool.tensor_tensor(sq[:, 2, :], sq[:, 2, :], sq[:, 3, :], ALU.add).then_inc(gstep, 1)
                    pool.wait_ge(gstep, 3 * n + 2)
                    pool.tensor_tensor(sq[:, 0, :], sq[:, 0, :], sq[:, 2, :], ALU.add).then_inc(gstep, 1)

            def mask(pair, u):
                c, jt, off = UNITS_OF[u]
                pool.wait_ge(exp_done, pair * UNITS + u + 1)
                tile = probs[:, u % PBUF, :, off:off + P]
                pool.tensor_tensor(tile, tile, causal[:, :, :], ALU.mult).then_inc(masked, 1)

            def add_probs(pair, u):
                c = UNITS_OF[u][0]
                pool.wait_ge(exp_done, pair * UNITS + u + 1)
                pool.wait_ge(summed, pair * UNITS + u)
                total = psums[:, rank[c] % 2, :, :]
                pool.tensor_tensor(total, total, probs[:, u % PBUF, :, :], ALU.add).then_inc(summed, 1)

            sum_squares(0)
            pool.wait_ge(y_turned, CHUNKS)
            pool.memset(yT[:, :], 0.0).then_inc(yT_cleared, 1)
            def slot(pair, u):
                if u in diag_rank:
                    mask(pair, u)
                if u in POOL_SUMS:
                    add_probs(pair, u)

            for s in range(ROT):
                slot(0, s)
            with pool.Fori(0, PAIRS - 1) as p:
                for s in range(ROT, ROT + UNITS):
                    slot(p + s // UNITS, s % UNITS)
            for s in range(ROT, UNITS):
                slot(PAIRS - 1, s)
            sum_squares(1)

        @block.vector
        def _(dve):
            steps = [0]

            def step(ins):
                steps[0] += 1
                ins.then_inc(vstep, 1)
                dve.wait_ge(vstep, steps[0])

            def statistics(c):
                for t in range(TPC * c, TPC * (c + 1)):
                    ins = dve.bn_stats(stats[:, t, :], X[:, t, :])
                step(ins)
                for t in range(TPC * c, TPC * (c + 1)):
                    ins = dve.bn_aggr(mv[:, t, :], stats[:, t, :])
                step(ins)

            def ask_roots(tiles, with_rms):
                step(dve.tensor_scalar(root_in[:, 0, tiles], mv[:, tiles, 1], LN_EPS, None, ALU.add))
                if with_rms:
                    step(dve.reciprocal(small[:, tiles], root_in[:, 0, tiles]))
                    step(dve.tensor_tensor(root_in[:, 1, tiles], small[:, tiles], mv[:, tiles, 1], ALU.mult))
                dve.sem_inc(root_asked, 1)

            def norm_scale(n, tiles, with_rms):
                dve.wait_ge(root_done, n + 1)
                if with_rms:
                    step(dve.scalar_tensor_tensor(small[:, tiles], root_out[:, 1, tiles], RMS_EPS,
                                                  root_out[:, 0, tiles], ALU.add, ALU.mult))
                    step(dve.reciprocal(scale_t[:, tiles], small[:, tiles]))
                else:
                    step(dve.reciprocal(scale_t[:, tiles], root_out[:, 0, tiles]))

            def normalise(k, r):
                n = CHUNKS * k + r
                if n >= 2:
                    dve.wait_ge(xn_turned, n - 1)
                for t in range(TPC):
                    i = TPC * ORDER[r] + t
                    ins = dve.tensor_scalar(xn[:, n % 2, t, :], X[:, i, :], mv[:, i, 0:1], scale_t[:, i:i + 1],
                                            ALU.subtract, ALU.mult)
                ins.then_inc(xn_ready, 1)

            def low_part(k, r):
                n = CHUNKS * k + r
                dve.wait_ge(xh_ready, n + 1)
                if r >= 2:
                    dve.wait_ge(up_done, FT * (n - 1))
                dve.tensor_tensor(xl[:, r % 2, :], TURN_BANK, xh[:, r % 2, :].bitcast(F32),
                                  ALU.subtract).then_inc(xl_ready, 1)

            def split_h(k, r, tiles=range(FT)):
                n = CHUNKS * k + r
                if r >= 2:
                    dve.wait_ge(down_done, n - 1)
                for f in tiles:
                    dve.wait_ge(gelu_done, FT * n + f + 1)
                    step(dve.tensor_copy(hh[r % 2][:, f, :], h[:, r % 2, f, :]))
                    dve.tensor_tensor(hl[r % 2][:, f, :], h[:, r % 2, f, :], hh[r % 2][:, f, :].bitcast(F32),
                                      ALU.subtract).then_inc(h_split, 1)

            def sum_last_squares(k):
                n = CHUNKS * k + CHUNKS - 1
                sq = hsq[1]
                dve.wait_ge(sq_done, FT * n + 2)
                dve.tensor_tensor(sq[:, 0, :], sq[:, 0, :], sq[:, 1, :], ALU.add)
                dve.wait_ge(sq_done, FT * n + 4)
                step(dve.tensor_tensor(sq[:, 2, :], sq[:, 2, :], sq[:, 3, :], ALU.add))
                dve.tensor_tensor(sq[:, 0, :], sq[:, 0, :], sq[:, 2, :], ALU.add).then_inc(last_sq_summed, 1)

            def down_scale(k, n_root):
                dve.wait_ge(ss_done, CHUNKS * (k + 1))
                dve.tensor_scalar(root_in[:, 0, :], SS_BANK[:, 0:TILES], 1.0 / F, None,
                                  ALU.mult).then_inc(root_asked, 1)
                dve.wait_ge(root_done, n_root + 1)
                step(dve.tensor_scalar(small[:, :], root_out[:, 0, :], RMS_EPS, 2.0, ALU.add, ALU.mult))
                step(dve.reciprocal(scale_t[:, :], small[:, :]))

            def update(k, r):
                dve.wait_ge(y_turned, CHUNKS * k + r + 1)
                for t in range(TPC):
                    i = TPC * ORDER[r] + t
                    ins = dve.scalar_tensor_tensor(X[:, i, :], psum[:, r, P * t:P * (t + 1)],
                                                   scale_t[:, i:i + 1], X[:, i, :], ALU.mult, ALU.add)
                ins.then_inc(x_updated, 1)

            for c in ORDER:
                dve.wait_ge(x_loaded[c], 16)
                statistics(c)
            every = slice(0, TILES)
            ask_roots(every, True)
            w = w_up_nat[:, :, :].rearrange("p t d -> p (t d)")
            dve.wait_ge(thr_ready, 2)
            step(dve.tensor_scalar(tern_neg[:, 0, :], w, thr[:, 2:3], None, ALU.is_lt))
            dve.scalar_tensor_tensor(w, w, thr[:, 0:1], tern_neg[:, 0, :], ALU.is_gt,
                                     ALU.subtract).then_inc(tern_up_ready, 1)
            norm_scale(0, every, True)
            normalise(0, 0)
            normalise(0, 1)
            low_part(0, 0)
            low_part(0, 1)
            normalise(0, 2)
            split_h(0, 0)
            low_part(0, 2)
            normalise(0, 3)
            split_h(0, 1)
            low_part(0, 3)
            split_h(0, 2)
            split_h(0, 3)

            def attention_scale(r):
                norm_scale(2 + r, tiles_of(r), False)
                dve.scalar_tensor_tensor(shift_t[:, tiles_of(r)], mv[:, tiles_of(r), 0], -1.0,
                                         scale_t[:, tiles_of(r)], ALU.mult, ALU.mult).then_inc(scale_ready, 1)

            def split(bank, c, T, chain, copied=None):
                cols = slice(CH * c, CH * (c + 1))
                lo, hi = slice(0, DH), slice(DH, P)
                if copied is not None:
                    dve.wait_ge(high_copied, copied)
                else:
                    dve.tensor_copy(T[lo, 0, cols], bank[lo, :])
                    dve.tensor_copy(T[hi, 1, cols], bank[hi, :]).then_inc(vchain, 1)
                    dve.wait_ge(vchain, chain + 1)
                dve.tensor_tensor(T[hi, 0, cols], bank[lo, :], T[lo, 0, cols].bitcast(F32), ALU.subtract)
                return dve.tensor_tensor(T[lo, 1, cols], bank[hi, :], T[hi, 1, cols].bitcast(F32), ALU.subtract)

            def last_use(pair, units):
                return (pair - 1) * UNITS + units

            def take(i, base, entry, pair, chain, first=False):
                _, kind, c, _ = entry
                bank = side(i, first)
                cols = slice(CH * c, CH * (c + 1))
                dve.wait_ge(side_done, base + i + 1)
                copied = 1 + SCALAR_HIGH.index(i) if first and i in SCALAR_HIGH else None
                if kind == "K":
                    if not first:
                        dve.wait_ge(scored, last_use(pair, first_unit[c] + TPC))
                    split(bank, c, K1, chain, copied).then_inc(side_taken, 1)
                elif kind == "Q":
                    if not first:
                        dve.wait_ge(scored, last_use(pair, last_unit[c] + 1))
                    split(bank, c, Qs, chain, copied).then_inc(side_taken, 1)
                elif kind == "V":
                    if not first:
                        dve.wait_ge(pv_done, last_use(pair, first_unit[c] + TPC))
                    dve.tensor_copy(V[:, TPC * c:TPC * (c + 1), :].rearrange("p t f -> p (t f)"),
                                    bank).then_inc(side_taken, 1)
                elif kind == "WT":
                    qk = bank[:, 0:2 * P].rearrange("p (i f) -> p i f", i=2)
                    dve.tensor_copy(WTh[:, :, :], qk).then_inc(vchain, 1)
                    dve.tensor_copy(WvT[:, :], bank[:, 2 * P:3 * P])
                    dve.wait_ge(vchain, chain + 1)
                    dve.tensor_tensor(WTl[:, :, :], qk, WTh[:, :, :].bitcast(F32), ALU.subtract).then_inc(side_taken, 1)
                elif kind == "xa":
                    dve.wait_ge(xah_stored, rank[c] + 1)
                    dve.wait_ge(xaT_stored, rank[c] + 1)
                    dve.tensor_tensor(xal[:, cols], bank, xah[:, cols].bitcast(F32), ALU.subtract).then_inc(side_taken, 1)
                elif kind == "fin":
                    x_c = X[:, TPC * c:TPC * (c + 1), :].rearrange("p t d -> p (t d)")
                    dve.tensor_tensor(x_c, bank, x_c, ALU.add).then_inc(side_taken, 1)
                    dve.wait_ge(side_taken, base + i + 1)
                    statistics(c)
                elif kind == "WoT":
                    dve.tensor_copy(WoT[:, :], bank[:, 0:P]).then_inc(side_taken, 1)
                elif kind == "den":
                    dve.transpose(den_t[:, :], bank).then_inc(side_taken, 1)
                    dve.wait_ge(side_taken, base + i + 1)
                    own = den_t[:, :].rearrange("p (b k) -> p b k", k=32)
                    dve.reciprocal(den_r[:, :], own[:, :, 0]).then_inc(vchain, 1)
                    dve.wait_ge(vchain, chain + 1)
                    dve.tensor_copy(den_b[:, :].rearrange("p (b k) -> p b k", k=32),
                                    den_r[:, :].unsqueeze(2).broadcast_to([P, CH // 32, 32])).then_inc(vchain, 1)
                    dve.wait_ge(vchain, chain + 2)
                    dve.transpose(rden[:, :], den_b[:, :]).then_inc(vchain, 1)
                    dve.wait_ge(vchain, chain + 3)
                    dve.wait_ge(pv_done, pair * UNITS + last_unit[c] + 1)
                    dve.tensor_tensor(OT[:, rank[c] % 2, :], O(rank[c]), rden[:, :], ALU.mult).then_inc(normed, 1)
                elif kind == "out":
                    dve.tensor_tensor(yT[:, cols], bank, yT[:, cols], ALU.add).then_inc(side_taken, 1)

            def add_probs(pair, u):
                c, jt, off = UNITS_OF[u]
                if u in POOL_SUMS:
                    return
                if u in diag_rank:
                    dve.wait_ge(masked, pair * DIAGS + diag_rank[u])
                else:
                    dve.wait_ge(exp_done, pair * UNITS + u + 1)
                dve.wait_ge(summed, pair * UNITS + u)
                total = psums[:, rank[c] % 2, :, off:CH]
                new = probs[:, u % PBUF, :, off:CH]
                if u == first_unit[c]:
                    dve.tensor_copy(total, new).then_inc(summed, 1)
                else:
                    dve.tensor_tensor(total, total, new, ALU.add).then_inc(summed, 1)

            def slot(pair, s, jobs, base, chain):
                if jobs is LAST_JOBS and s == UNITS - 2:
                    norm_scale(6, late, True)
                    dve.scalar_tensor_tensor(shift_t[:, late], mv[:, late, 0], -1.0, scale_t[:, late], ALU.mult,
                                             ALU.mult).then_inc(scale_ready, 1)
                for i, e in enumerate(jobs):
                    if e[0] == s:
                        take(i, base, e, pair + 1 if e[3] else pair, chain + chain_before(jobs, i))
                if jobs is LAST_JOBS and s == UNITS - 3:
                    ask_roots(late, True)
                u = s + AHEAD
                if u < UNITS:
                    add_probs(pair, u)
                elif jobs is not LAST_JOBS:
                    add_probs(pair + 1, u - UNITS)

            def first_take(i):
                take(i, 0, FIRST_JOBS[i], 0, chain_before(FIRST_JOBS, i), first=True)

            sum_last_squares(0)
            first_take(WT_JOB)
            down_scale(0, 1)
            for r in range(CHUNKS):
                if r == CHUNKS - 1:
                    first_take(XA3_JOB)
                update(0, r)
                if r > 0:
                    attention_scale(r - 1)
                dve.wait_ge(x_updated, r + 1)
                statistics(ORDER[r])
                ask_roots(tiles_of(r), False)
            first_take(XA2_JOB)
            attention_scale(CHUNKS - 1)

            late, early = slice(2 * TPC, TILES), slice(0, 2 * TPC)
            for s in range(-1, ROT):
                for i, e in enumerate(FIRST_JOBS):
                    if e[0] == s and i > XA2_JOB:
                        first_take(i)
                if s == -1:
                    for u in range(AHEAD):
                        add_probs(0, u)
                else:
                    add_probs(0, s + AHEAD)
            dve.wait_ge(yT_cleared, 1)
            with dve.Fori(0, PAIRS - 1) as p:
                for s in range(ROT, ROT + UNITS):
                    slot(p, s, JOBS, p * NJ + NFJ, p * NC + NFC)
            for s in range(ROT, UNITS):
                slot(PAIRS - 1, s, LAST_JOBS, (PAIRS - 1) * NJ + NFJ, (PAIRS - 1) * NC + NFC)

            def tail_take(kind, c):
                i = next(i for i, e in enumerate(LAST_JOBS) if e[1:3] == (kind, c))
                take(i, (PAIRS - 1) * NJ + NFJ, LAST_JOBS[i], PAIRS - 1,
                     (PAIRS - 1) * NC + NFC + chain_before(LAST_JOBS, i))

            low_part(1, 0)
            tail_take("den", 0)
            tail_take("out", 1)
            tail_take("fin", 1)
            tail_take("out", 0)
            low_part(1, 1)
            split_h(1, 0, range(1))
            tail_take("fin", 0)
            ask_roots(early, True)
            split_h(1, 0, range(1, FT))
            norm_scale(7, early, True)
            normalise(1, 2)
            split_h(1, 1, range(2))
            low_part(1, 2)
            normalise(1, 3)
            split_h(1, 1, range(2, FT))
            low_part(1, 3)
            split_h(1, 2)
            split_h(1, 3)
            sum_last_squares(1)
            down_scale(1, 8)
            for r in range(CHUNKS):
                update(1, r)


_INS = ["L0_attn_x", "L0_attn_Wq", "L0_attn_Wk", "L0_attn_Wv", "L0_attn_Wo", "L0_ffn_w_up", "L0_ffn_w_down"]


def kernel(**inputs):
    import numpy as _np
    import concourse.bacc as _bacc
    from concourse import mybir as _mybir
    from concourse.bass_utils import run_bass_kernel_spmd as _run

    nc = _bacc.Bacc("TRN2", target_bir_lowering=False, num_devices=1)
    arrays, args = {}, []
    for name in _INS:
        a = _np.ascontiguousarray(inputs[name])
        arrays[f"in_{name}_dram"] = a
        args.append(nc.dram_tensor(f"in_{name}_dram", a.shape, _mybir.dt.from_np(a.dtype), kind="ExternalInput").ap())
    shape = tuple(inputs["L0_attn_x"].shape)
    args.append(nc.dram_tensor("out_0_dram", shape, _mybir.dt.float32, kind="ExternalOutput").ap())
    bass_macaron_block(nc, *args)
    r = _run(nc, [arrays], core_ids=[0])
    return r.results[0]["out_0_dram"]
```
